# Optimizing a Trainium2 kernel written in Bass

```python
import numpy as np
import jax
import jax.numpy as jnp

def _softmax(x, axis=-1):
    return jax.nn.softmax(x, axis=axis)

def _gelu(x):
    return jax.nn.gelu(x, approximate=True)

def _silu(x):
    return jax.nn.silu(x)

def _sigmoid(x):
    return jax.nn.sigmoid(x)

def _layernorm(x, axis=-1, eps=1e-05):
    m = jnp.mean(x, axis=axis, keepdims=True)
    v = jnp.var(x, axis=axis, keepdims=True)
    return (x - m) / jnp.sqrt(v + eps)

def _scatter_add(tgt, idx, src, axis=0):
    return tgt.at[idx].add(src)

def _segment_sum(src, seg, n):
    return jax.ops.segment_sum(src, seg, n)
kernel_name = 'mk_prb_d1_jaxref_r4_b30741'

def setup_inputs(seed: int=0):
    np.random.seed(seed)
    _w = jnp.asarray

    def _L0_attn_setup():
        import jax, jax.numpy as jnp
        import numpy as np
        import math
        D_MODEL = 256
        NUM_HEADS = 16

        def alibi_slopes(num_heads):
            x = (2 ** 8) ** (1.0 / num_heads)
            return jnp.array([1.0 / x ** (i + 1) for i in range(num_heads)], dtype=jnp.float32)
        key = jax.random.key(seed)
        k1, k2 = jax.random.split(key)
        x = jax.random.normal(k1, (4, 512, D_MODEL), dtype=jnp.float32)
        W_kqv = jax.random.normal(k2, (3 * D_MODEL, D_MODEL), dtype=jnp.float32) * (1.0 / math.sqrt(D_MODEL))
        return {'x': x, 'W_kqv': W_kqv}
    _L0_attn_in = _L0_attn_setup()

    def _L0_ffn_setup():
        import jax, jax.numpy as jnp
        import numpy as np
        B, S, D = (1, 512, 256)
        E, K, F = (8, 2, 352)
        NS = 2
        SCALE = 2.5

        def _swiglu_mlp(x, wg, wu, wd):
            return jax.nn.silu(x @ wg) * (x @ wu) @ wd
        key = jax.random.key(seed)
        ks = jax.random.split(key, 8)
        s = 0.02
        return {'hidden_states': jax.random.normal(ks[0], (B, S, D), jnp.float32), 'gate_w': jax.random.normal(ks[1], (E, D), jnp.float32) * s, 'w_gate': jax.random.normal(ks[2], (E, D, F), jnp.float32) * s, 'w_up': jax.random.normal(ks[3], (E, D, F), jnp.float32) * s, 'w_down': jax.random.normal(ks[4], (E, F, D), jnp.float32) * s, 'sw_gate': jax.random.normal(ks[5], (D, F * NS), jnp.float32) * s, 'sw_up': jax.random.normal(ks[6], (D, F * NS), jnp.float32) * s, 'sw_down': jax.random.normal(ks[7], (F * NS, D), jnp.float32) * s}
    _L0_ffn_in = _L0_ffn_setup()
    _d = {'L0_attn_x': _L0_attn_in['x'], 'L0_attn_W_kqv': _L0_attn_in['W_kqv'], 'L0_ffn_gate_w': _L0_ffn_in['gate_w'], 'L0_ffn_w_gate': _L0_ffn_in['w_gate'], 'L0_ffn_w_up': _L0_ffn_in['w_up'], 'L0_ffn_w_down': _L0_ffn_in['w_down'], 'L0_ffn_sw_gate': _L0_ffn_in['sw_gate'], 'L0_ffn_sw_up': _L0_ffn_in['sw_up'], 'L0_ffn_sw_down': _L0_ffn_in['sw_down']}
    _x0 = _d['L0_attn_x']
    _d['L0_attn_x'] = jax.random.normal(jax.random.fold_in(jax.random.key(seed), 1), (8, 1024, 256), dtype=_x0.dtype)
    del _x0
    return _d

def reference(L0_attn_x, L0_attn_W_kqv, L0_ffn_gate_w, L0_ffn_w_gate, L0_ffn_w_up, L0_ffn_w_down, L0_ffn_sw_gate, L0_ffn_sw_up, L0_ffn_sw_down):

    def _L0_attn_ref(x, W_kqv):
        import jax, jax.numpy as jnp
        import numpy as np
        import math
        D_MODEL = 256
        NUM_HEADS = 16

        def alibi_slopes(num_heads):
            x = (2 ** 8) ** (1.0 / num_heads)
            return jnp.array([1.0 / x ** (i + 1) for i in range(num_heads)], dtype=jnp.float32)
        B, S, D = x.shape
        H = NUM_HEADS
        hd = D // H
        scale = math.sqrt(D)
        kqv = x @ W_kqv.T
        k_, q_, v_ = jnp.split(kqv, 3, axis=-1)
        q = q_.reshape(B, S, H, hd).transpose(0, 2, 1, 3)
        k = k_.reshape(B, S, H, hd).transpose(0, 2, 1, 3)
        v = v_.reshape(B, S, H, hd).transpose(0, 2, 1, 3)
        pos = jnp.arange(S)
        rel = pos[None, :] - pos[:, None]
        bias = alibi_slopes(H)[:, None, None] * rel.astype(jnp.float32)
        score = jnp.einsum('bhsd,bhnd->bhsn', q, k) / scale + bias[None]
        attn = jax.nn.softmax(score, axis=-1)
        out = jnp.einsum('bhsn,bhnd->bhsd', attn, v)
        return out.transpose(0, 2, 1, 3).reshape(B, S, D)

    def _L0_ffn_ref(hidden_states, gate_w, w_gate, w_up, w_down, sw_gate, sw_up, sw_down):
        import jax, jax.numpy as jnp
        import numpy as np
        B, S, D = (1, 512, 256)
        E, K, F = (8, 2, 352)
        NS = 2
        SCALE = 2.5

        def _swiglu_mlp(x, wg, wu, wd):
            return jax.nn.silu(x @ wg) * (x @ wu) @ wd
        identity = hidden_states
        x = hidden_states.reshape(-1, hidden_states.shape[-1])
        T = x.shape[0]
        logits = x.astype(jnp.float32) @ gate_w.astype(jnp.float32).T
        scores = jax.nn.softmax(logits, axis=-1)
        topk_w, topk_i = jax.lax.top_k(scores, K)
        topk_w = topk_w / (topk_w.sum(-1, keepdims=True) + 1e-20) * SCALE
        combine = jnp.zeros((T, E), jnp.float32).at[jnp.arange(T)[:, None], topk_i].set(topk_w)
        g = jax.nn.silu(jnp.einsum('td,edf->etf', x, w_gate)) * jnp.einsum('td,edf->etf', x, w_up)
        expert_out = jnp.einsum('etf,efd->etd', g, w_down)
        y = jnp.einsum('te,etd->td', combine, expert_out).astype(x.dtype)
        y = y.reshape(identity.shape)
        return y + _swiglu_mlp(identity, sw_gate, sw_up, sw_down)
    x = L0_attn_x
    xn = _layernorm(x, axis=-1)
    x = x + _L0_attn_ref(xn, L0_attn_W_kqv) + _L0_ffn_ref(xn, L0_ffn_gate_w, L0_ffn_w_gate, L0_ffn_w_up, L0_ffn_w_down, L0_ffn_sw_gate, L0_ffn_sw_up, L0_ffn_sw_down)
    return x

_drawn_inputs = setup_inputs


def setup_inputs(seed=0):
    import zlib

    import numpy as np

    out = dict(_drawn_inputs(seed))
    spreads = {}
    factors = {}
    for name, (base, spread) in spreads.items():
        noise = np.random.default_rng([zlib.crc32(name.encode()), seed]).standard_normal(out[name].shape)
        drawn = base * np.exp(spread * noise) if base else spread * noise
        out[name] = jnp.asarray(drawn.astype(out[name].dtype))
    for name, factor in factors.items():
        out[name] = (out[name] * factor).astype(out[name].dtype)
    return out
```

```python
from contextlib import ExitStack

import numpy as np
import concourse.bass as bass
from concourse import mybir

F32 = mybir.dt.float32
F32R = mybir.dt.float32r
I32 = mybir.dt.int32
ALU = mybir.AluOpType
ACT = mybir.ActivationFunctionType
AX = mybir.AxisListType
ds = bass.ds

P = 128
B, S, D = 8, 1024, 256
T = B * S
H, HD = 16, 16
E, F = 8, 352
NS = 2
EA = E + NS
KD = D // P
FC = [128, 128, 96]
NBLK = T // P
TT = 512
TB = TT // P
NT = T // TT
MOE_TILES = 2 * T // P + E
EPS = 1e-5
ROUTE_SCALE = 2.5
GROUPS = B * H // 4
GH = 4
NK = S // P
QR = 4 * HD
S1_ROWS = QR + 2
S2_ROWS = QR + 3


def hold(eng, sem, value, passed):
    eng.wait_ge(sem, value).then_inc(passed, 1)


class Chain:

    def __init__(self, eng, sem, base=0, passed=None):
        self.eng, self.sem, self.base, self.passed, self.k = eng, sem, base, passed, 0

    def link(self, ins):
        ins.then_inc(self.sem, 1)
        self.k += 1
        if self.passed is None:
            self.eng.wait_ge(self.sem, self.base + self.k)
        else:
            hold(self.eng, self.sem, self.base + self.k, self.passed)


def steps(eng, n, unroll, emit):
    turns = (n - 2) // unroll
    emit(0, 0, 0, True, n == 1)
    with eng.Fori(0, turns) as i:
        for u in range(unroll):
            emit(i * unroll + (1 + u), (1 + u) % unroll, i + (1 + u) // unroll, False, False)
    for j in range(1 + turns * unroll, n):
        emit(j, j % unroll, j // unroll, False, j == n - 1)


def build(nc, x, wqkv, gate_wt, w_gate, w_up, w_down, sw_gate, sw_up, sw_down, ident_in, tri_in, ali, out):
    with ExitStack() as kernel_ctx:
        def dram(name, shape, dt=F32):
            return nc.dram_tensor(name, shape, dt, kind="Internal").ap()

        scratch = dict(
            xn=dram("xn_scratch", [T, D]),
            qk=dram("qk_scratch", [2, 2 * D, T]),
            v=dram("v_scratch", [T, D]),
            lists=dram("lists_scratch", [E * T, 1], I32),
            ali=dram("ali_scratch", [H + 1, 2, S]),
            credit=dram("credit_scratch", [2, P, 1]),
            ysh=dram("ysh_scratch", [T, D]),
            yr=dram("yr_scratch", [MOE_TILES * P, D]),
        )

        def sb(name, shape, dt=F32):
            return kernel_ctx.enter_context(nc.sbuf_tensor(name, shape, dt))

        keep = dict(
            ident=sb("ident", [P, P]),
            logits=sb("logits", [P, NBLK * E]),
            pick=sb("pick", [P, 2, NBLK]),
            slot=sb("slot", [P, 2, NBLK]),
            count=sb("count", [P, E]),
            em8=sb("em8", [P, E]),
        )
        project(nc, keep, scratch, x, wqkv, gate_wt, ident_in, tri_in, ali)
        experts(nc, keep, scratch, w_gate, w_up, w_down, sw_gate, sw_up, sw_down)
        attend(nc, keep, scratch, x, out)


def stage(nc, ctx):
    def sb(name, shape, dt=F32):
        return ctx.enter_context(nc.sbuf_tensor(name, shape, dt))

    def ps(name, shape, dt=F32):
        return ctx.enter_context(nc.psum_tensor(name, shape, dt))

    def sem(name):
        return ctx.enter_context(nc.semaphore(name))

    return sb, ps, sem


def project(nc, keep, scratch, x, wqkv, gate_wt, ident_in, tri_in, ali):
    with ExitStack() as ctx:
        sb, ps, sem = stage(nc, ctx)
        ident, logits, pick, slot, count, em8 = (keep[k] for k in ("ident", "logits", "pick", "slot", "count", "em8"))
        w32 = sb("w32", [P, KD, 3 * D])
        w_hi, w_lo = sb("w_hi", [P, KD, 3 * D], F32R), sb("w_lo", [P, KD, 3 * D], F32R)
        g32 = sb("g32", [P, KD, E])
        g_hi, g_lo = sb("g_hi", [P, KD, E], F32R), sb("g_lo", [P, KD, E], F32R)
        tri, ones = sb("tri", [P, P]), sb("ones", [P, P])
        zeros = sb("zeros", [P, E * T // P], I32)
        x_sb = [sb(f"x{i}", [P, TB, D]) for i in range(2)]
        xn = [sb(f"xn{i}", [P, TB, D]) for i in range(2)]
        xt_hi = [sb(f"xt_hi{i}", [P, KD, TT], F32R) for i in range(2)]
        xt_lo = [sb(f"xt_lo{i}", [P, KD, TT], F32R) for i in range(2)]
        qk_out = [sb(f"qk_out{i}", [P, 2, 4, TT], F32R) for i in range(2)]
        v_out = [sb(f"v_out{i}", [P, TB, D]) for i in range(2)]
        stats, mv = sb("stats", [P, TB, 6]), sb("mv", [P, TB, 2])
        ve, root, newt, half = sb("ve", [P, TB]), sb("root", [P, TB]), sb("newt", [P, TB]), sb("half", [P, TB])
        lt, cmp_a, cmp_b = sb("lt", [P, TB, E]), sb("cmp_a", [P, TB, E]), sb("cmp_b", [P, TB, E])
        top, idx = sb("top", [P, TB]), sb("idx", [P, 2, TB])
        chosen, pos, run = sb("chosen", [P, 2, TB, E]), sb("pos", [P, TB, E]), sb("run", [P, TB + 1, E])
        both = sb("both", [P, TB, E])
        region = sb("region", [P, E])
        sl = sb("sl", [P, 2, TB])
        slot_i = sb("slot_i", [P, 2, TB], I32)
        token_all = sb("token_all", [P, NBLK], I32)
        token = sb("token", [P, TB], I32)

        p_xt = ps("p_xt", [P, KD, TT])
        p_qk = [ps(f"p_qk{i}", [P, TT]) for i in range(2)]
        p_v = ps("p_v", [P, TB, D])
        p_g = ps("p_g", [P, TT])

        names = ("w_in ali_st const_in iota_done x_in0 x_in1 ve_ready pow_ready xn_ready xt_ps xt_hi_ok xt_lo_ok "
                 "qk_ps qk_hi_ok qk_lo_ok v_ps v_ok g_ps g_read m_ready cnt_ps slot_ready tok_ok "
                 "passed xn_st0 xn_st1 qk_st0 qk_st1 v_st0 v_st1 scat zero_st dve_ln dve_sel dve_pro pool_pro")
        s = {n: sem("a_" + n) for n in names.split()}

        block = ctx.enter_context(nc.Block())

        @block.sync
        def _(sp):
            sp.dma_start(w32[:], wqkv.rearrange("(k p) n -> p k n", p=P)).then_inc(s["w_in"], 16)
            sp.dma_start(g32[:], gate_wt.rearrange("(k p) e -> p k e", p=P)).then_inc(s["w_in"], 16)
            sp.dma_start(ident[:], ident_in).then_inc(s["const_in"], 16)
            sp.dma_start(tri[:], tri_in).then_inc(s["const_in"], 16)
            sp.dma_start(scratch["ali"], ali).then_inc(s["ali_st"], 16)
            for i in range(2):
                sp.sem_inc(s[f"xn_st{i}"], 16)
                sp.sem_inc(s[f"qk_st{i}"], 16)
                sp.sem_inc(s[f"v_st{i}"], 16)
            xr = x.rearrange("(n b p) d -> n p b d", p=P, b=TB)
            xnr = scratch["xn"].rearrange("(n b p) d -> n p b d", p=P, b=TB)
            vr = scratch["v"].rearrange("(n b p) d -> n p b d", p=P, b=TB)

            def load(n, u):
                sp.dma_start(x_sb[u][:], xr[n]).then_inc(s[f"x_in{u}"], 16)

            load(0, 0)

            def tile(n, u, turn, first, last):
                if not last:
                    if not first:
                        sp.wait_ge(s["xn_ready"], n)
                    nn = 1 if first else n + 1
                    sp.dma_start(x_sb[1 - u][:], xr[ds(nn, 1)].rearrange("o p b d -> p (o b) d")
                                 if not isinstance(nn, int) else xr[nn]).then_inc(s[f"x_in{1 - u}"], 16)
                pick_n = (lambda a: a[n]) if isinstance(n, int) else (lambda a: a[ds(n, 1)].rearrange("o p b d -> p (o b) d"))
                sp.wait_ge(s["xn_ready"], n + 1)
                sp.dma_start(pick_n(xnr), xn[u][:]).then_inc(s[f"xn_st{u}"], 16)
                sp.wait_ge(s["qk_lo_ok"], 4 * n + 4)
                for hl in range(2):
                    sp.dma_start(scratch["qk"][hl].rearrange("(c p) t -> p c t", p=P)[:, :, ds(n * TT, TT)],
                                 qk_out[u][:, hl].bitcast(F32)).then_inc(s[f"qk_st{u}"], 16)
                sp.wait_ge(s["v_ok"], n + 1)
                sp.dma_start(pick_n(vr), v_out[u][:]).then_inc(s[f"v_st{u}"], 16)

            steps(sp, NT, 2, tile)
            for i in range(2):
                sp.wait_ge(s[f"xn_st{i}"], 16 * (NT // 2 + 1))
                sp.wait_ge(s[f"qk_st{i}"], 32 * (NT // 2) + 16)
                sp.wait_ge(s[f"v_st{i}"], 16 * (NT // 2 + 1))
            sp.wait_ge(s["scat"], 16 * 2 * NBLK)
            sp.wait_ge(s["ali_st"], 16)

        @block.gpsimd
        def _(pool):
            g = nc.gpsimd
            g.memset(ones[:], 1.0).then_inc(s["iota_done"], 1)
            g.memset(half[:], -0.5).then_inc(s["iota_done"], 1)
            g.iota(em8[:], [[1, E]], base=-E, channel_multiplier=0,
                   allow_small_or_imprecise_dtypes=True).then_inc(s["iota_done"], 1)
            g.iota(region[:], [[T, E]], base=0, channel_multiplier=0,
                   allow_small_or_imprecise_dtypes=True).then_inc(s["iota_done"], 1)
            g.iota(token_all[:], [[P, NBLK]], base=0, channel_multiplier=1).then_inc(s["iota_done"], 1)
            g.memset(zeros[:], 0).then_inc(s["pool_pro"], 1)
            pool.wait_ge(s["pool_pro"], 1)
            g.dma_start(scratch["lists"].rearrange("(p n) o -> p (n o)", p=P), zeros[:]).then_inc(s["zero_st"], 16)
            pool.wait_ge(s["iota_done"], 5)

            def power(n):
                hold(pool, s["ve_ready"], n + 1, s["passed"])
                g.tensor_tensor(root[:], ve[:], half[:], ALU.pow).then_inc(s["pow_ready"], 1)

            power(0)

            def tile(n, u, turn, first, last):
                if not last:
                    power(n + 1)
                if not first:
                    hold(pool, s["scat"], n * (16 * 2 * TB), s["passed"])
                g.tensor_copy(token[:], token_all[:, ds(n * TB, TB)]).then_inc(s["tok_ok"], 1)
                hold(pool, s["tok_ok"], n + 1, s["passed"])
                hold(pool, s["slot_ready"], n + 1, s["passed"])
                if first:
                    pool.wait_ge(s["zero_st"], 16)
                for c in range(2):
                    for b in range(TB):
                        g.indirect_dma_start(
                            scratch["lists"], bass.IndirectOffsetOnAxis(slot_i[:, c, b:b + 1], 0),
                            token[:, b:b + 1], None).then_inc(s["scat"], 16)

            steps(pool, NT, 2, tile)

        @block.vector
        def _(dve):
            v = nc.vector
            pro = Chain(dve, s["dve_pro"])
            dve.wait_ge(s["w_in"], 32)
            pro.link(v.tensor_copy(w_hi[:], w32[:]))
            pro.link(v.tensor_copy(g_hi[:], g32[:]))
            pro.link(v.tensor_tensor(w_lo[:], w32[:], w_hi[:].bitcast(F32), ALU.subtract))
            pro.link(v.tensor_tensor(g_lo[:], g32[:], g_hi[:].bitcast(F32), ALU.subtract))
            pro.link(v.memset(run[:], 0.0))
            dve.wait_ge(s["iota_done"], 5)

            LN_LINKS = 6

            def layernorm(n, u, turn):
                c = Chain(dve, s["dve_ln"], n * LN_LINKS, s["passed"])
                dve.wait_ge(s[f"x_in{u}"], 16 * (turn + 1))
                for b in range(TB):
                    last = v.bn_stats(stats[:, b], x_sb[u][:, b])
                c.link(last)
                for b in range(TB):
                    last = v.bn_aggr(mv[:, b], stats[:, b])
                c.link(last)
                v.tensor_scalar(ve[:], mv[:, :, 1], EPS, None, ALU.add).then_inc(s["ve_ready"], 1)
                dve.wait_ge(s["pow_ready"], n + 1)
                c.link(v.tensor_tensor(newt[:], root[:], root[:], ALU.mult))
                c.link(v.tensor_tensor(newt[:], newt[:], ve[:], ALU.mult))
                c.link(v.tensor_scalar(newt[:], newt[:], -0.5, 1.5, ALU.mult, ALU.add))
                c.link(v.tensor_tensor(newt[:], newt[:], root[:], ALU.mult))
                dve.wait_ge(s[f"xn_st{u}"], 16 * (turn + 1))
                for b in range(TB):
                    last = v.tensor_scalar(xn[u][:, b], x_sb[u][:, b], mv[:, b, 0:1], newt[:, b:b + 1],
                                           ALU.subtract, ALU.mult)
                last.then_inc(s["xn_ready"], 1)
                assert c.k == LN_LINKS

            layernorm(0, 0, 0)
            SEL_LINKS = 24

            def choose(n, u, first):
                c = Chain(dve, s["dve_sel"], n * SEL_LINKS)
                dve.wait_ge(s["g_ps"], n + 1)
                lp = p_g[:, 0:TB * E].rearrange("p (b e) -> p b e", b=TB)
                v.tensor_copy(logits[:, ds(n * TB * E, TB * E)], p_g[:, 0:TB * E])
                c.link(v.tensor_copy(lt[:], lp))
                em = em8[:, None, :].to_broadcast([P, TB, E])

                def pick_top(src, k):
                    c.link(v.tensor_reduce(top[:], src, AX.X, ALU.max))
                    c.link(v.tensor_tensor(cmp_a[:], src, top[:, :, None].to_broadcast([P, TB, E]), ALU.is_equal))
                    c.link(v.tensor_tensor(cmp_b[:], cmp_a[:], em, ALU.mult))
                    c.link(v.tensor_reduce(idx[:, k], cmp_b[:], AX.X, ALU.min))
                    c.link(v.tensor_tensor(chosen[:, k], em, idx[:, k, :, None].to_broadcast([P, TB, E]), ALU.is_equal))

                pick_top(lt[:], 0)
                c.link(v.scalar_tensor_tensor(lt[:], chosen[:, 0], -1e30, lt[:], ALU.mult, ALU.add))
                pick_top(lt[:], 1)
                v.tensor_copy(pick[:, :, ds(n * TB, TB)], idx[:])
                v.tensor_tensor(both[:], chosen[:, 0], chosen[:, 1], ALU.add).then_inc(s["m_ready"], 1)
                dve.wait_ge(s["cnt_ps"], n + 1)
                before = p_g[:, 64:64 + TB * E].rearrange("p (b e) -> p b e", b=TB)
                total = p_g[:, 128:128 + TB * E].rearrange("p (b e) -> p b e", b=TB)
                for b in range(TB):
                    c.link(v.tensor_tensor(run[:, b + 1], run[:, b], total[:, b], ALU.add))
                c.link(v.tensor_tensor(pos[:], before, run[:, 0:TB], ALU.add))
                c.link(v.tensor_copy(run[:, 0], run[:, TB]))
                c.link(v.tensor_tensor(pos[:], pos[:], region[:, None, :].to_broadcast([P, TB, E]), ALU.add))
                for k in range(2):
                    c.link(v.tensor_tensor(cmp_a[:], pos[:], chosen[:, k], ALU.mult))
                    c.link(v.tensor_reduce(sl[:, k], cmp_a[:], AX.X, ALU.add))
                v.tensor_copy(slot[:, :, ds(n * TB, TB)], sl[:])
                if not first:
                    dve.wait_ge(s["scat"], n * (16 * 2 * TB))
                c.link(v.tensor_copy(slot_i[:], sl[:]))
                v.tensor_copy(count[:], run[:, 0]).then_inc(s["slot_ready"], 1)
                assert c.k == SEL_LINKS

            def tile(n, u, turn, first, last):
                dve.wait_ge(s["xt_hi_ok"], n + 1)
                v.tensor_tensor(xt_lo[u][:], p_xt[:], xt_hi[u][:].bitcast(F32), ALU.subtract).then_inc(s["xt_lo_ok"], 1)
                if not last:
                    layernorm(n + 1, 1 - u, turn if u == 0 else turn + 1)
                for c in range(4):
                    dve.wait_ge(s["qk_hi_ok"], 4 * n + c + 1)
                    v.scalar_tensor_tensor(qk_out[u][:, 1, c], p_qk[c % 2][:], 1.0 if c < 2 else 1 / 16,
                                           qk_out[u][:, 0, c].bitcast(F32), ALU.mult,
                                           ALU.subtract).then_inc(s["qk_lo_ok"], 1)
                choose(n, u, first)

            steps(dve, NT, 2, tile)

        @block.scalar
        def _(act):
            a = nc.scalar

            def tile(n, u, turn, first, last):
                act.wait_ge(s["xt_ps"], n + 1)
                a.copy(xt_hi[u][:], p_xt[:]).then_inc(s["xt_hi_ok"], 1)
                act.wait_ge(s[f"qk_st{u}"], 32 * turn + 16)
                for c in range(4):
                    act.wait_ge(s["qk_ps"], 4 * n + c + 1)
                    a.mul(qk_out[u][:, 0, c], p_qk[c % 2][:], 1.0 if c < 2 else 1 / 16).then_inc(s["qk_hi_ok"], 1)
                act.wait_ge(s[f"v_st{u}"], 16 * (turn + 1))
                act.wait_ge(s["v_ps"], n + 1)
                a.copy(v_out[u][:], p_v[:]).then_inc(s["v_ok"], 1)

            steps(act, NT, 2, tile)

        @block.tensor
        def _(pe):
            t = nc.tensor
            pe.wait_ge(s["const_in"], 32)
            pe.wait_ge(s["iota_done"], 5)
            pe.wait_ge(s["dve_pro"], 4)

            def turn_x(n, u):
                pe.wait_ge(s["xn_ready"], n + 1)
                for b in range(TB):
                    for k in range(KD):
                        last = t.transpose(p_xt[:, k, b * P:(b + 1) * P], xn[u][:, b, k * P:(k + 1) * P], ident[:])
                last.then_inc(s["xt_ps"], 1)

            turn_x(0, 0)

            def products(dst, lhs, rhs):
                n = 0
                for k in range(KD):
                    for a, b in ((0, 0), (0, 1), (1, 0)):
                        last = t.matmul(dst, lhs[a](k), rhs[b](k), start=(n == 0), stop=(n == 3 * KD - 1))
                        n += 1
                return last

            def tile(n, u, turn, first, last):
                pe.wait_ge(s["xt_lo_ok"], n + 1)
                if not last:
                    turn_x(n + 1, 1 - u)
                for c in range(4):
                    if not (first and c < 2):
                        pe.wait_ge(s["qk_lo_ok"], 4 * n + c - 1)
                    products(p_qk[c % 2][:], [lambda k, w=w: w[:, k, c * P:(c + 1) * P] for w in (w_hi, w_lo)],
                             [lambda k, w=w: w[u][:, k] for w in (xt_hi, xt_lo)]).then_inc(s["qk_ps"], 1)
                xs = lambda b: [lambda k, w=w: w[u][:, k, b * P:(b + 1) * P] for w in (xt_hi, xt_lo)]
                if not first:
                    pe.wait_ge(s["slot_ready"], n)
                for b in range(TB):
                    ins = products(p_g[:, b * E:(b + 1) * E], xs(b), [lambda k, w=w: w[:, k] for w in (g_hi, g_lo)])
                ins.then_inc(s["g_ps"], 1)
                if not first:
                    pe.wait_ge(s["v_ok"], n)
                for b in range(TB):
                    ins = products(p_v[:, b], xs(b), [lambda k, w=w: w[:, k, 2 * D:3 * D] for w in (w_hi, w_lo)])
                ins.then_inc(s["v_ps"], 1)
                pe.wait_ge(s["m_ready"], n + 1)
                t.matmul(p_g[:, 64:64 + TB * E], tri[:], both[:].rearrange("p b e -> p (b e)"), start=True, stop=True)
                t.matmul(p_g[:, 128:128 + TB * E], ones[:], both[:].rearrange("p b e -> p (b e)"),
                         start=True, stop=True).then_inc(s["cnt_ps"], 1)

            steps(pe, NT, 2, tile)


def experts(nc, keep, scratch, w_gate, w_up, w_down, sw_gate, sw_up, sw_down):
    with ExitStack() as ctx:
        sb, ps, sem = stage(nc, ctx)
        ident, count = keep["ident"], keep["count"]
        GU, DN = 2 * F, len(FC) * D
        wgu = [sb(f"wgu_{h}", [P, KD * EA * GU], F32R) for h in ("hi", "lo")]
        wdn = [sb(f"wdn_{h}", [P, EA * DN], F32R) for h in ("hi", "lo")]
        gu32 = sb("gu32", [P, KD, GU])
        dn32 = sb("dn32", [P, DN])
        XB = 4
        x_sb = [sb(f"xe{i}", [P, D]) for i in range(XB)]
        ids = [sb(f"ids{i}", [P, 1], I32) for i in range(XB)]
        xt = [[sb(f"xet_{h}{i}", [P, KD, P], F32R) for i in range(2)] for h in ("hi", "lo")]
        gated, h_sb = sb("gated", [P, F]), sb("h_sb", [P, F])
        ht = [[sb(f"ht_{h}{i}", [P, 3, P], F32R) for i in range(2)] for h in ("hi", "lo")]
        y_sb = [sb(f"y{i}", [P, D]) for i in range(4)]
        tile_no = sb("tile_no", [1, MOE_TILES])
        t_exp, t_cmp, t_blk = sb("t_exp", [1, MOE_TILES]), sb("t_cmp", [1, MOE_TILES]), sb("t_blk", [1, MOE_TILES])
        w_off_i, blk_i = sb("w_off_i", [1, 2, MOE_TILES], I32), sb("blk_i", [1, MOE_TILES], I32)
        nt_i, nt_f = sb("nt_i", [P, E], I32), sb("nt_f", [P, E])
        base, end, one8 = sb("base", [P, E]), sb("end", [P, E]), sb("one8", [P, E])
        adj = sb("adj", [P, E])
        yslot = sb("yslot", [P, 2, NBLK])
        keep_slot, pick = keep["slot"], keep["pick"]

        p_x = ps("pe_x", [P, KD, P])
        p_gate, p_up = ps("p_gate", [P, 512]), ps("p_up", [P, 512])
        p_h, p_y = ps("pe_h", [P, 3, P]), ps("pe_y", [P, 512])

        names = ("passed gu_in split tab tiles_ready pool_pro")
        s = {n: sem("e_" + n) for n in names.split()}

        block = ctx.enter_context(nc.Block())

        def gu_at(half_, k, e_off, up, n=F):
            return wgu[half_][:, ds(e_off + (k * EA * GU + up * F), n)]

        order = [8, 9] + list(range(8))

        def stream(name):
            ns = ("x_in0 x_in1 x_in2 x_in3 id_in0 id_in1 id_in2 id_in3 xt_ps xt_hi xt_lo gu_ps gated h_ok "
                  "ht_ps ht_hi ht_lo y_ps y_free y_st0 y_st1 y_st2 y_st3")
            return {n: sem(f"{name}_{n}") for n in ns.split()}

        sh, rt = stream("sh"), stream("rt")

        def io(eng, q, n, src, dst, ids_of=None):
            def load(j, u, free):
                if free is not None:
                    eng.wait_ge(q["xt_ps"], free)
                if ids_of is None:
                    eng.dma_start(x_sb[u][:], src[ds(j * P, P)]).then_inc(q[f"x_in{u}"], 16)
                else:
                    blk = eng.value_load(ids_of[0:1, ds(j, 1)], min_val=0, max_val=E * T // P - 1)
                    eng.dma_start(ids[u][:], src[ds(blk * P, P)]).then_inc(q[f"id_in{u}"], 16)

            for i in range(XB):
                eng.sem_inc(q[f"y_st{i}"], 16)
            for j in range(XB - 1):
                load(j, j, None)

            def step(j, u, turn, first, last):
                if isinstance(j, int) and j > 4:
                    if j + XB - 1 < n:
                        load(j + XB - 1, (u + XB - 1) % XB, j)
                else:
                    load(j + XB - 1, (u + XB - 1) % XB, None if first else j)
                eng.wait_ge(q["y_free"], j + 2)
                eng.dma_start(dst[ds(j * P, P)], y_sb[u][:]).then_inc(q[f"y_st{u}"], 16)

            steps_tail(eng, n, XB, step)
            for i in range(XB):
                eng.wait_ge(q[f"y_st{i}"], 16 * (n // XB + 1))

        def steps_tail(eng, n, unroll, emit):
            turns = (n - unroll) // unroll
            emit(0, 0, 0, True, False)
            with eng.Fori(0, turns) as i:
                for u in range(unroll):
                    emit(i * unroll + (1 + u), (1 + u) % unroll, i + (1 + u) // unroll, False, False)
            for j in range(1 + turns * unroll, n):
                emit(j, j % unroll, j // unroll, False, j == n - 1)

        @block.gpsimd
        def _(pool):
            g = nc.gpsimd
            g.memset(one8[:], 1.0).then_inc(s["pool_pro"], 1)
            g.iota(tile_no[:], [[1, MOE_TILES]], base=0, channel_multiplier=0,
                   allow_small_or_imprecise_dtypes=True).then_inc(s["pool_pro"], 1)
            k = 0
            for n, e in enumerate(order):
                hold(pool, s["gu_in"], 64 * (n + 1), s["passed"])
                wg = [w[:].rearrange("p (k e f) -> p k e f", k=KD, e=EA)[:, :, e] for w in wgu]
                g.tensor_copy(wg[0], gu32[:]).then_inc(s["pool_pro"], 1)
                dv = [[w[0:r, e * DN + c0:e * DN + c1] for w in wdn] + [dn32[0:r, c0:c1]]
                      for r, c0, c1 in ((P, 0, 2 * D), (FC[2], 2 * D, 3 * D))]
                for hi, lo, src in dv:
                    g.tensor_copy(hi, src).then_inc(s["pool_pro"], 1)
                k += 3
                pool.wait_ge(s["pool_pro"], 2 + k)
                g.tensor_tensor(wg[1], gu32[:], wg[0].bitcast(F32), ALU.subtract).then_inc(s["pool_pro"], 1)
                for hi, lo, src in dv:
                    g.tensor_tensor(lo, src, hi.bitcast(F32), ALU.subtract).then_inc(s["pool_pro"], 1)
                k += 3
                pool.wait_ge(s["pool_pro"], 2 + k)
                pool.sem_inc(s["split"], 1)
            def step(j, u, turn, first, last):
                hold(pool, rt[f"id_in{u}"], 16 * (turn + 1), s["passed"])
                g.indirect_dma_start(x_sb[u][:], None, scratch["xn"],
                                     bass.IndirectOffsetOnAxis(ids[u][:], 0)).then_inc(rt[f"x_in{u}"], 16)
            steps(pool, MOE_TILES, XB, step)

        def pe_stream(pe, q, n, subs, offsets, tiles):
            t = nc.tensor

            def turn_x(j, u, turn):
                pe.wait_ge(q[f"x_in{u}"], 16 * (turn + 1))
                for k in range(KD):
                    last = t.transpose(p_x[:, k], x_sb[u][:, k * P:(k + 1) * P], ident[:])
                last.then_inc(q["xt_ps"], 1)

            def down(job, par, group, sub, off):
                pe.wait_ge(q["ht_lo"], job + 1)
                if sub == 0:
                    pe.wait_ge(q["y_free"], group + 1)
                i, all_ = 0, 3 * len(FC)
                for c, rows in enumerate(FC):
                    for a, b in ((0, 0), (0, 1), (1, 0)):
                        last = t.matmul(p_y[:, 0:D], ht[a][par][0:rows, c], wdn[b][0:rows, ds(off + c * D, D)],
                                        start=(i == 0 and sub == 0), stop=(i == all_ - 1 and sub == subs - 1))
                        i += 1
                if sub == subs - 1:
                    last.then_inc(q["y_ps"], 1)

            held = {}

            def step(j, u, turn, first, last):
                par = u % 2
                if first:
                    turn_x(0, 0, 0)
                offs = offsets(pe, j)
                prev = held.get("prev")
                pe.wait_ge(q["xt_lo"], j + 1)
                for sub in range(subs):
                    job = subs * j + sub
                    jp = job_parity(subs, par, sub)
                    gu_off, dn_off = offs[sub]
                    for up, dst in ((0, p_gate), (1, p_up)):
                        i = 0
                        for k in range(KD):
                            for a, b in ((0, 0), (0, 1), (1, 0)):
                                ins = t.matmul(dst[:, 0:F], xt[a][par][:, k], gu_at(b, k, gu_off, up),
                                               start=(i == 0), stop=(i == 3 * KD - 1))
                                i += 1
                    ins.then_inc(q["gu_ps"], 1)
                    if not (first and sub == 0):
                        if sub == 0:
                            down(job - 1, 1 - jp, j - 1, subs - 1, prev_off(pe, j, subs))
                        else:
                            down(job - 1, 1 - jp, j, sub - 1, offs[sub - 1][1])
                    if sub == 0 and not last:
                        turn_x(j + 1, (u + 1) % XB, turn + (1 if u == XB - 1 else 0))
                    pe.wait_ge(q["h_ok"], job + 1)
                    for c, rows in enumerate(FC):
                        ins = t.transpose(p_h[0:rows, c], h_sb[:, c * P:c * P + rows], ident[:])
                    ins.then_inc(q["ht_ps"], 1)
                if last:
                    down(subs * j + subs - 1, job_parity(subs, par, subs - 1), j, subs - 1, offs[subs - 1][1])

            def prev_off(pe, j, subs):
                return tiles(pe, j)

            steps(pe, n, XB, step)

        def job_parity(subs, par, sub):
            return par if subs == 1 else sub

        def act_stream(act, q, n, subs):
            a = nc.scalar

            def split_x(j, par):
                act.wait_ge(q["xt_ps"], j + 1)
                a.copy(xt[0][par][:], p_x[:]).then_inc(q["xt_hi"], 1)

            def step(j, u, turn, first, last):
                par = u % 2
                if first:
                    split_x(0, 0)
                for sub in range(subs):
                    job = subs * j + sub
                    act.wait_ge(q["gu_ps"], job + 1)
                    a.activation(gated[:], p_gate[:, 0:F], ACT.Silu).then_inc(q["gated"], 1)
                    if sub == 0 and not last:
                        split_x(j + 1, 1 - par)
                    act.wait_ge(q["ht_ps"], job + 1)
                    jp = job_parity(subs, par, sub)
                    a.copy(ht[0][jp][:, 0:2], p_h[:, 0:2])
                    a.copy(ht[0][jp][0:FC[2], 2], p_h[0:FC[2], 2]).then_inc(q["ht_hi"], 1)

            steps(act, n, XB, step)

        def dve_stream(dve, q, n, subs):
            v = nc.vector

            def split_x(j, par):
                dve.wait_ge(q["xt_hi"], j + 1)
                v.tensor_tensor(xt[1][par][:], p_x[:], xt[0][par][:].bitcast(F32), ALU.subtract).then_inc(q["xt_lo"], 1)

            def finish(j, u, turn):
                dve.wait_ge(q["y_ps"], j + 1)
                dve.wait_ge(q[f"y_st{u}"], 16 * (turn + 1))
                v.tensor_copy(y_sb[u][:], p_y[:, 0:D]).then_inc(q["y_free"], 1)

            dve.sem_inc(q["y_free"], 1)

            def step(j, u, turn, first, last):
                par = u % 2
                if first:
                    split_x(0, 0)
                for sub in range(subs):
                    job = subs * j + sub
                    dve.wait_ge(q["gated"], job + 1)
                    v.tensor_tensor(h_sb[:], p_up[:, 0:F], gated[:], ALU.mult).then_inc(q["h_ok"], 1)
                    if sub == 0 and not first:
                        finish(j - 1, (u - 1) % XB, turn - (1 if u == 0 else 0))
                    if sub == 0 and not last:
                        split_x(j + 1, 1 - par)
                    dve.wait_ge(q["ht_hi"], job + 1)
                    jp = job_parity(subs, par, sub)
                    v.tensor_tensor(ht[1][jp][:, 0:2], p_h[:, 0:2], ht[0][jp][:, 0:2].bitcast(F32), ALU.subtract)
                    v.tensor_tensor(ht[1][jp][0:FC[2], 2], p_h[0:FC[2], 2], ht[0][jp][0:FC[2], 2].bitcast(F32),
                                    ALU.subtract).then_inc(q["ht_lo"], 1)
                if last:
                    finish(j, u, turn)

            steps(dve, n, XB, step)

        @block.sync
        def _(sp):
            for n, e in enumerate(order):
                if n:
                    sp.wait_ge(s["split"], n)
                if e < E:
                    g, u, d = w_gate[e], w_up[e], w_down[e]
                else:
                    cols = slice((e - E) * F, (e - E + 1) * F)
                    g, u, d = sw_gate[:, cols], sw_up[:, cols], sw_down[cols]
                sp.dma_start(gu32[:, :, 0:F], g.rearrange("(k p) f -> p k f", p=P)).then_inc(s["gu_in"], 16)
                sp.dma_start(gu32[:, :, F:2 * F], u.rearrange("(k p) f -> p k f", p=P)).then_inc(s["gu_in"], 16)
                sp.dma_start(dn32[:, 0:2 * D].rearrange("p (c d) -> p c d", c=2),
                             d[0:2 * P].rearrange("(c p) d -> p c d", p=P)).then_inc(s["gu_in"], 16)
                sp.dma_start(dn32[0:FC[2], 2 * D:3 * D], d[2 * P:F]).then_inc(s["gu_in"], 16)
            io(sp, sh, NBLK, scratch["xn"], scratch["ysh"])
            sp.wait_ge(s["tiles_ready"], 1)
            io(sp, rt, MOE_TILES, scratch["lists"], scratch["yr"], blk_i)

        @block.vector
        def _(dve):
            v = nc.vector
            c = Chain(dve, s["tab"])
            dve.wait_ge(s["pool_pro"], 2)
            c.link(v.tensor_scalar(nt_f[:], count[:], float(P - 1), None, ALU.add))
            c.link(v.tensor_copy(nt_i[:], nt_f[:]))
            c.link(v.tensor_scalar(nt_i[:], nt_i[:], 7, None, ALU.arith_shift_right))
            c.link(v.tensor_copy(nt_f[:], nt_i[:]))
            c.link(v.tensor_tensor_scan(end[:], one8[:], nt_f[:], 0.0, ALU.mult, ALU.add))
            c.link(v.tensor_tensor(base[:], end[:], nt_f[:], ALU.subtract))
            c.link(v.tensor_scalar(t_exp[:], tile_no[:], end[0:1, 0:1], None, ALU.is_ge))
            for e in range(1, E - 1):
                c.link(v.scalar_tensor_tensor(t_exp[:], tile_no[:], end[0:1, e:e + 1], t_exp[:], ALU.is_ge, ALU.add))
            c.link(v.tensor_copy(t_blk[:], tile_no[:]))
            for e in range(E):
                c.link(v.tensor_scalar(adj[:, e:e + 1], base[:, e:e + 1], -1.0, float(e * T // P), ALU.mult, ALU.add))
                c.link(v.tensor_scalar(t_cmp[:], t_exp[:], float(e), adj[0:1, e:e + 1], ALU.is_equal, ALU.mult))
                c.link(v.tensor_tensor(t_blk[:], t_blk[:], t_cmp[:], ALU.add))
            c.link(v.tensor_scalar(blk_i[:], t_blk[:], float(E * T // P - 1), None, ALU.min))
            c.link(v.tensor_scalar(w_off_i[:, 0], t_exp[:], float(GU), None, ALU.mult))
            c.link(v.tensor_scalar(w_off_i[:, 1], t_exp[:], float(DN), None, ALU.mult))
            c.link(v.tensor_copy(yslot[:], keep_slot[:]))
            for e in range(E):
                c.link(v.tensor_scalar(base[:, e:e + 1], adj[:, e:e + 1], float(-P), None, ALU.mult))
                for k in range(2):
                    c.link(v.tensor_scalar(keep_slot[:, k], pick[:, k], float(e - E), base[:, e:e + 1],
                                           ALU.is_equal, ALU.mult))
                    c.link(v.tensor_tensor(yslot[:, k], yslot[:, k], keep_slot[:, k], ALU.add))
            v.tensor_copy(keep_slot[:], yslot[:]).then_inc(s["tiles_ready"], 1)
            dve_stream(dve, sh, NBLK, NS)
            dve_stream(dve, rt, MOE_TILES, 1)

        @block.scalar
        def _(act):
            act_stream(act, sh, NBLK, NS)
            act_stream(act, rt, MOE_TILES, 1)

        @block.tensor
        def _(pe):
            pe.wait_ge(s["split"], NS)
            shared = [((E + i) * GU, (E + i) * DN) for i in range(NS)]
            pe_stream(pe, sh, NBLK, NS, lambda pe, j: shared, lambda pe, j: shared[-1][1])
            pe.wait_ge(s["split"], EA)
            pe.wait_ge(s["tiles_ready"], 1)

            def offsets(pe, j):
                gu = pe.value_load(w_off_i[0:1, 0, ds(j, 1)], min_val=0, max_val=(E - 1) * GU)
                dn = pe.value_load(w_off_i[0:1, 1, ds(j, 1)], min_val=0, max_val=(E - 1) * DN)
                return [(gu, dn)]

            def before(pe, j):
                return pe.value_load(w_off_i[0:1, 1, ds(j - 1, 1)], min_val=0, max_val=(E - 1) * DN)

            pe_stream(pe, rt, MOE_TILES, 1, offsets, before)


def attend(nc, keep, scratch, x, out):
    with ExitStack() as ctx:
        sb, ps, sem = stage(nc, ctx)
        ident, logits, pick, slot, em8 = (keep[k] for k in ("ident", "logits", "pick", "slot", "em8"))
        GS = GH * S
        k_op = [sb(f"k_op{i}", [S2_ROWS, GH, S], F32R) for i in range(2)]
        q_op = [sb(f"q_op{i}", [96, GH, S], F32R) for i in range(2)]
        v_in = [sb(f"v_in{i}", [P, NK, GH * HD]) for i in range(2)]
        v_op = [sb(f"v_op{i}", [P, NK, GH, 32]) for i in range(2)]
        probs = [sb(f"probs{i}", [P, GH, S]) for i in range(3)]
        mx = sb("mx", [P, NK, 2])
        neg = sb("neg", [P, NK], F32R)
        m_row = [sb(f"m_row{i}", [NK, P], F32R) for i in range(2)]
        o_sb = sb("o_sb", [P, 2, 512])
        rec = sb("rec", [P, 4, GH, HD])
        att = sb("att", [P, 2 * NK, D])
        xc = [sb(f"xc{i}", [P, D]) for i in range(2)]
        yc = [sb(f"yc{i}", [P, D]) for i in range(2)]
        y1 = [sb(f"y1{i}", [P, D]) for i in range(2)]
        y2 = [sb(f"y2{i}", [P, D]) for i in range(2)]
        oc = [sb(f"oc{i}", [P, D]) for i in range(2)]
        slot_i = sb("yslot_i", [P, 2, NBLK], I32)
        col_i = [sb(f"col_i{i}", [P, 2], I32) for i in range(2)]
        col_w = [sb(f"col_w{i}", [P, 2]) for i in range(2)]
        wts = sb("wts", [P, 2, NBLK])
        ex, cmp_ = sb("ex", [P, NBLK, E]), sb("cmp_", [P, NBLK, E])
        t64, z64 = sb("t64", [P, NBLK]), sb("z64", [P, NBLK])

        p1 = [ps(f"p1_{i}", [P, 512]) for i in range(2)]
        p2 = [ps(f"p2_{i}", [P, 2, 512]) for i in range(2)]
        p_o = ps("p_o", [P, 2, 512])

        names = ("passed k_in0 k_in1 v_in0 v_in1 ones_in init s1_ps s1_read m_ok m_in00 m_in01 m_in02 m_in03 m_in10 m_in11 m_in12 m_in13 s2_ps p_ok pv_done v_ok "
                 "o_ps o_ok att_ok sub_ok ex_ok w_ready dve_w dve_g pool_c xc_in0 xc_in1 yg_in0 yg_in1 col_ok o_st0 o_st1 c_ok")
        s = {n: sem("t_" + n) for n in names.split()}

        block = ctx.enter_context(nc.Block())
        U1 = GH * (NK * 2 + 1) + 2
        assert U1 % 2 == 0

        def groups(eng, emit):
            with eng.Fori(0, GROUPS // 2 - 1) as i:
                emit(i * 2, 0, i, True)
                emit(i * 2 + 1, 1, i, True)
            emit(GROUPS - 2, 0, GROUPS // 2 - 1, True)
            emit(GROUPS - 1, 1, GROUPS // 2 - 1, False)

        ORDER = ([(kb, h) for kb in range(2) for h in range(GH - 1)] + [(kb, GH - 1) for kb in range(2)]
                 + [(kb, h) for kb in range(2, NK) for h in range(GH)])

        @block.sync
        def _(sp):
            qk, ali = scratch["qk"], scratch["ali"]
            sp.wait_ge(s["init"], 4)
            for i in range(2):
                sp.dma_start(k_op[i][QR + 2:QR + 3].bitcast(F32),
                             ali[H:H + 1, 0:1].to_broadcast([1, GH, S])).then_inc(s["ones_in"], 16)

            def load(g, u, b, hg):
                for base, op, parts in ((0, k_op, (0, 1, 0, 1)), (D, q_op, (0, 0, 1, 1))):
                    for r, hl in enumerate(parts):
                        sp.dma_start(op[u][r * HD:(r + 1) * HD].bitcast(F32),
                                     qk[hl][ds(hg * (GH * HD) + base, GH * HD), ds(b * S, S)]
                                     .rearrange("(h d) t -> d h t", d=HD)).then_inc(s[f"k_in{u}"], 16)
                sp.dma_start(k_op[u][QR:QR + 2].bitcast(F32),
                             ali[ds(hg * GH, GH)].rearrange("h a t -> a h t")).then_inc(s[f"k_in{u}"], 16)
                sp.dma_start(v_in[u][:], scratch["v"][ds(b * S, S), ds(hg * (GH * HD), GH * HD)]
                             .rearrange("(k p) c -> p k c", p=P)).then_inc(s[f"v_in{u}"], 16)

            def send_max(g, h, u):
                sp.wait_ge(s["m_ok"], g * GH + (h + 1))
                sp.dma_start(q_op[u][QR + 2:QR + 3, h].rearrange("o (q c) -> o q c", q=NK).bitcast(F32),
                             m_row[h % 2][:].bitcast(F32)).then_inc(s[f"m_in{u}{h}"], 16)

            load(0, 0, 0, 0)
            for h in range(GH):
                send_max(0, h, 0)

            def group(g, u, turn, has_next):
                if has_next:
                    if not (isinstance(g, int) and g == 0):
                        pass
                    sp.wait_ge(s["pv_done"], g * NK + NK_CREDIT)
                    nxt = g + 1
                    if isinstance(nxt, int):
                        load(nxt, 1 - u, nxt // (H // GH), nxt % (H // GH))
                    else:
                        load(nxt, 1 - u, nxt // (H // GH), nxt % (H // GH))
                    for h in range(GH):
                        send_max(nxt, h, 1 - u)

            NK_CREDIT = NK
            groups(sp, group)

        @block.gpsimd
        def _(pool):
            g_ = nc.gpsimd
            for i in range(2):
                g_.memset(q_op[i][QR:96].bitcast(F32), 1.0).then_inc(s["init"], 1)
                pool.wait_ge(s["init"], 2 * i + 1)
                g_.memset(v_op[i][:], 1.0).then_inc(s["init"], 1)
                pool.wait_ge(s["init"], 2 * i + 2)
            pool.sem_inc(s["pv_done"], NK)

            def spread_v(g, u, turn):
                hold(pool, s[f"v_in{u}"], 16 * (turn + 1), s["passed"])
                g_.tensor_copy(v_op[u][:, :, :, 0:HD],
                               v_in[u][:].rearrange("p k (h d) -> p k h d", h=GH)).then_inc(s["v_ok"], 1)

            pool.wait_ge(s["init"], 4)
            spread_v(0, 0, 0)
            g_.tensor_copy(slot_i[:], slot[:]).then_inc(s["pool_c"], 1)
            pool.wait_ge(s["pool_c"], 1)
            pool.wait_ge(s["w_ready"], 1)
            for i in range(2):
                pool.dma_start(scratch["credit"][i], wts[:, 0, 0:1]).then_inc(s[f"o_st{i}"], 16)

            CPB = 8

            def combine(n, u, turn, ring):
                c = Chain(pool, s["pool_c"], n * CPB + 1, s["passed"])
                pool.dma_start(xc[u][:], x[ds(n * P, P)]).then_inc(s[f"xc_in{u}"], 16)
                pool.dma_start(yc[u][:], scratch["ysh"][ds(n * P, P)]).then_inc(s[f"xc_in{u}"], 16)
                c.link(g_.tensor_copy(col_w[u][:], wts[:, :, ds(n, 1)].rearrange("p a o -> p (a o)")))
                c.link(g_.tensor_copy(col_i[u][:], slot_i[:, :, ds(n, 1)].rearrange("p a o -> p (a o)")))
                for k, y in enumerate((y1, y2)):
                    g_.indirect_dma_start(y[u][:], None, scratch["yr"],
                                          bass.IndirectOffsetOnAxis(col_i[u][:, k:k + 1], 0)).then_inc(s[f"yg_in{u}"], 16)
                hold(pool, s[f"xc_in{u}"], 32 * (turn + 1), s["passed"])
                hold(pool, s[f"o_st{u}"], 16 * (turn + 1), s["passed"])
                c.link(g_.tensor_tensor(oc[u][:], xc[u][:], yc[u][:], ALU.add))
                c.link(g_.tensor_tensor(oc[u][:], oc[u][:], att[:, ds(ring, 1)].rearrange("p o d -> p (o d)"), ALU.add))
                hold(pool, s[f"yg_in{u}"], 32 * (turn + 1), s["passed"])
                for k, y in enumerate((y1, y2)):
                    c.link(g_.tensor_scalar(y[u][:], y[u][:], col_w[u][:, k:k + 1], None, ALU.mult))
                    c.link(g_.tensor_tensor(oc[u][:], oc[u][:], y[u][:], ALU.add))
                assert c.k == CPB
                pool.sem_inc(s["c_ok"], 1)
                pool.dma_start(out[ds(n * P, P)], oc[u][:]).then_inc(s[f"o_st{u}"], 16)

            pool.wait_ge(s["w_ready"], 1)
            GB = H // GH

            def batch(b, last):
                for hg in range(GB):
                    u = hg % 2
                    if not (last and hg == GB - 1):
                        hold(pool, s["pv_done"], (b * GB + hg) * NK + NK, s["passed"])
                        spread_v(b * GB + hg + 1, 1 - u, b * 2 + (hg + 1) // 2)
                    if hg == 1 and not (isinstance(b, int) and b == 0):
                        blocks(b - 1)
                if last:
                    blocks(b)

            def blocks(b):
                hold(pool, s["att_ok"], b * (GB * 2) + GB * 2, s["passed"])
                with pool.Fori(0, NK // 2) as i:
                    for u in range(2):
                        combine(b * NK + i * 2 + u, u, b * (NK // 2) + i, (b % 2) * NK + i * 2 + u)

            batch(0, False)
            with pool.Fori(1, B - 1) as b:
                batch(b, False)
            batch(B - 1, True)
            for i in range(2):
                pool.wait_ge(s[f"o_st{i}"], 16 * (NBLK // 2 + 1))

        @block.vector
        def _(dve):
            v = nc.vector
            c = Chain(dve, s["dve_w"])
            lg = logits[:].rearrange("p (n e) -> p n e", e=E)
            wide = lambda a: a[:, :, None].to_broadcast([P, NBLK, E])
            c.link(v.tensor_reduce(t64[:], lg, AX.X, ALU.max))
            c.link(v.tensor_tensor(ex[:], lg, wide(t64), ALU.subtract))
            v.tensor_copy(cmp_[:, 0:1], ex[:, 0:1]).then_inc(s["sub_ok"], 1)
            dve.wait_ge(s["ex_ok"], 1)
            c.link(v.tensor_reduce(z64[:], ex[:], AX.X, ALU.add))
            c.link(v.reciprocal(t64[:], z64[:]))
            c.link(v.tensor_tensor(ex[:], ex[:], wide(t64), ALU.mult))
            em = em8[:, None, :].to_broadcast([P, NBLK, E])
            for k in range(2):
                c.link(v.tensor_tensor(cmp_[:], em, wide(pick[:, k]), ALU.is_equal))
                c.link(v.tensor_tensor(cmp_[:], cmp_[:], ex[:], ALU.mult))
                c.link(v.tensor_reduce(wts[:, k], cmp_[:], AX.X, ALU.add))
            c.link(v.tensor_tensor(t64[:], wts[:, 0], wts[:, 1], ALU.add))
            c.link(v.tensor_scalar(t64[:], t64[:], 1e-20, None, ALU.add))
            c.link(v.reciprocal(z64[:], t64[:]))
            for k in range(2):
                ins = v.scalar_tensor_tensor(wts[:, k], wts[:, k], ROUTE_SCALE, z64[:], ALU.mult, ALU.mult)
            ins.then_inc(s["w_ready"], 1)

            dve.sem_inc(s["c_ok"], 2 * NK)
            dve.sem_inc(s["s1_read"], 2)
            LK = GH * 2 + 2
            def s1_unit(g, base, turn, unit, u):
                h, w = divmod(unit, 2 * NK + 1)
                use = base + unit
                dve.wait_ge(s["s1_ps"], use + 1)
                if w < 2 * NK:
                    v.tensor_reduce(mx[:, w // 2, w % 2:w % 2 + 1], p1[unit % 2][:], AX.X, ALU.max).then_inc(s["s1_read"], 1)
                    if w == 2 * NK - 1:
                        dve.wait_ge(s["s1_read"], use + 3)
                        v.tensor_reduce(neg[:], mx[:], AX.X, ALU.max, negate=True).then_inc(s["dve_g"], 1)
                else:
                    if h >= 2:
                        dve.wait_ge(s[f"m_in{u}{h - 2}"], 16 * (turn + 1))
                    v.tensor_copy(m_row[h % 2][:], p1[unit % 2][0:NK, 0:P]).then_inc(s["m_ok"], 1)
                    dve.wait_ge(s["m_ok"], g * GH + (h + 1))
                    dve.sem_inc(s["s1_read"], 1)

            for unit in range(GH * (2 * NK + 1)):
                s1_unit(0, 0, 0, unit, 0)

            SU = GH * (2 * NK + 1)
            def group(g, u, turn, has_next):
                base = g * U1 + SU
                if has_next:
                    nt = turn if u == 0 else turn + 1
                    for h in (2, 3):
                        dve.wait_ge(s[f"m_in{u}{h}"], 16 * (turn + 1))
                    for unit in range(SU):
                        s1_unit(g + 1, base, nt, unit, 1 - u)
                extra = SU if has_next else 0
                dve.wait_ge(s["pv_done"], g * NK + 2 * NK)
                v.tensor_copy(o_sb[:], p_o[:]).then_inc(s["o_ok"], 1)
                for half in range(2):
                    use = base + extra + half
                    dve.wait_ge(s["s1_ps"], use + 1)
                    ot = p1[(extra + half) % 2][:].rearrange("p (q h c) -> p q h c", q=4, h=GH)
                    v.reciprocal(rec[:], ot[:, :, :, HD:2 * HD]).then_inc(s["dve_g"], 1)
                    dve.wait_ge(s["dve_g"], (g + 1) * GH + g * 2 + (half + 1) + (GH if has_next else 0))
                    b, hg = g // (H // GH), g % (H // GH)
                    dve.wait_ge(s["c_ok"], b * NK + NK)
                    dst = att[:, ds((b % 2) * NK + 4 * half, 4), ds(hg * (GH * HD), GH * HD)]
                    v.tensor_tensor(dst.rearrange("p q (h c) -> p q h c", h=GH), ot[:, :, :, 0:HD], rec[:],
                                    ALU.mult).then_inc(s["att_ok"], 1)
                    dve.wait_ge(s["att_ok"], g * 2 + half + 1)
                    dve.sem_inc(s["s1_read"], 1)

            groups(dve, group)

        @block.scalar
        def _(act):
            a = nc.scalar
            act.wait_ge(s["sub_ok"], 1)
            a.activation(ex[:], ex[:], ACT.Exp).then_inc(s["ex_ok"], 1)
            act.sem_inc(s["p_ok"], 2)

            def group(g, u, turn, has_next):
                for n, (kb, h) in enumerate(ORDER):
                    i = g * (GH * NK) + n
                    act.wait_ge(s["s2_ps"], i + 1)
                    act.wait_ge(s["pv_done"], g * NK + (NK - 1 if kb == 0 else NK if kb < 3 else NK + kb - 2))
                    a.activation(probs[kb % 3][:, h], p2[n % 2][:].rearrange("p a c -> p (a c)"),
                                 ACT.Exp).then_inc(s["p_ok"], 1)

            groups(act, group)

        LAST = {kb: max(n for n, (k, _) in enumerate(ORDER) if k == kb) for kb in range(NK)}
        PV_AFTER = {LAST[kb] + 2: kb for kb in range(NK - 1)}

        @block.tensor
        def _(pe):
            t = nc.tensor

            def s1_unit(g, base, unit, u, turn):
                h, w = divmod(unit, 2 * NK + 1)
                use = base + unit
                pe.wait_ge(s["s1_read"], use + 1)
                if w < 2 * NK:
                    qb, half = divmod(w, 2)
                    ins = t.matmul(p1[unit % 2][:], q_op[u][0:S1_ROWS, h, qb * P:(qb + 1) * P],
                                   k_op[u][0:S1_ROWS, h, half * 512:(half + 1) * 512], start=True, stop=True)
                else:
                    pe.wait_ge(s["dve_g"], neg_count(g, h))
                    ins = t.transpose(p1[unit % 2][0:NK, 0:P], neg[:].bitcast(F32), ident[:])
                ins.then_inc(s["s1_ps"], 1)

            def neg_count(g, h):
                if isinstance(g, int) and g == 0:
                    return h + 1
                return g * GH + (g - 1) * 2 + (h + 1)

            def s2_unit(g, u, turn, n, kb, h):
                i = g * (GH * NK) + n
                pe.wait_ge(s["p_ok"], i + 1)
                if kb == 0:
                    pe.wait_ge(s[f"m_in{u}{h}"], 16 * (turn + 1))
                for half in range(2):
                    ins = t.matmul(p2[n % 2][:, half], k_op[u][0:S2_ROWS, h, kb * P:(kb + 1) * P],
                                   q_op[u][0:S2_ROWS, h, half * 512:(half + 1) * 512], start=True, stop=True)
                ins.then_inc(s["s2_ps"], 1)

            def pv(g, u, kb):
                pe.wait_ge(s["p_ok"], g * (GH * NK) + (LAST[kb] + 3))
                if kb == 0:
                    pe.wait_ge(s["v_ok"], g + 1)
                    pe.wait_ge(s["o_ok"], g + 1)
                for half in range(2):
                    for h in range(GH):
                        ins = t.matmul(p_o[32 * h:32 * h + 32, half], v_op[u][:, kb, h],
                                       probs[kb % 3][:, h, half * 512:(half + 1) * 512],
                                       start=(kb == 0), stop=(kb == NK - 1))
                ins.then_inc(s["pv_done"], 1)

            pe.sem_inc(s["o_ok"], 1)
            pe.wait_ge(s["ones_in"], 32)
            pe.wait_ge(s["k_in0"], 16 * 9)
            for unit in range(GH * (2 * NK + 1)):
                s1_unit(0, 0, unit, 0, 0)

            SU = GH * (2 * NK + 1)

            def group(g, u, turn, has_next):
                base = g * U1 + SU
                if has_next:
                    nt = turn if u == 0 else turn + 1
                s1 = 0
                for n, (kb, h) in enumerate(ORDER):
                    s2_unit(g, u, turn, n, kb, h)
                    if has_next:
                        if n == 2:
                            pe.wait_ge(s[f"k_in{1 - u}"], (nt + 1) * (16 * 9))
                        want = SU * (n - 1) // (GH * NK - 2) if n >= 2 else 0
                        while s1 < want:
                            s1_unit(g + 1, base, s1, 1 - u, nt)
                            s1 += 1
                    if n in PV_AFTER:
                        pv(g, u, PV_AFTER[n])
                pv(g, u, NK - 1)
                extra = SU if has_next else 0
                assert not has_next or s1 == SU
                pe.wait_ge(s["o_ok"], g + 2)
                for half in range(2):
                    use = base + extra + half
                    pe.wait_ge(s["s1_read"], use + 1)
                    for q in range(4):
                        ins = t.transpose(p1[(extra + half) % 2][:, q * P:(q + 1) * P],
                                          o_sb[:, half, q * P:(q + 1) * P], ident[:])
                    ins.then_inc(s["s1_ps"], 1)

            groups(pe, group)


def kernel(L0_attn_x, L0_attn_W_kqv, L0_ffn_gate_w, L0_ffn_w_gate, L0_ffn_w_up, L0_ffn_w_down,
           L0_ffn_sw_gate, L0_ffn_sw_up, L0_ffn_sw_down):
    import concourse.bacc as bacc
    from concourse.bass_utils import run_bass_kernel_spmd

    f32 = np.float32
    ratio = (2 ** 8) ** (1.0 / H)
    slopes = np.array([1.0 / ratio ** (i + 1) for i in range(H)], dtype=f32)
    bias = slopes[:, None] * (np.arange(S) - (S - 1)).astype(f32)[None, :]
    top = (bias.view(np.uint32) & np.uint32(0xFFFFF000)).view(f32)
    ali = np.zeros((H + 1, 2, S), f32)
    ali[:H, 0], ali[:H, 1], ali[H] = top, bias - top, 1.0
    arrays = {
        "x": np.ascontiguousarray(L0_attn_x).reshape(T, D),
        "wqkv": np.ascontiguousarray(np.asarray(L0_attn_W_kqv).T),
        "gate_wt": np.ascontiguousarray(np.asarray(L0_ffn_gate_w).T),
        "w_gate": np.ascontiguousarray(L0_ffn_w_gate),
        "w_up": np.ascontiguousarray(L0_ffn_w_up),
        "w_down": np.ascontiguousarray(L0_ffn_w_down),
        "sw_gate": np.ascontiguousarray(L0_ffn_sw_gate),
        "sw_up": np.ascontiguousarray(L0_ffn_sw_up),
        "sw_down": np.ascontiguousarray(L0_ffn_sw_down),
        "ident": np.eye(P, dtype=f32),
        "tri": np.triu(np.ones((P, P), f32), 1),
        "ali": ali,
    }
    nc = bacc.Bacc("TRN2", target_bir_lowering=False, num_devices=1)
    args = [nc.dram_tensor(f"in_{k}", a.shape, mybir.dt.from_np(a.dtype), kind="ExternalInput").ap()
            for k, a in arrays.items()]
    out = nc.dram_tensor("out_0", (T, D), F32, kind="ExternalOutput").ap()
    build(nc, *args, out)
    r = run_bass_kernel_spmd(nc, [{f"in_{k}": a for k, a in arrays.items()}], core_ids=[0])
    return r.results[0]["out_0"].reshape(B, S, D)
```

```python
from contextlib import ExitStack

import numpy as np
import concourse.bass as bass
from concourse import mybir

F32 = mybir.dt.float32
F32R = mybir.dt.float32r
I32 = mybir.dt.int32
ALU = mybir.AluOpType
ACT = mybir.ActivationFunctionType
AX = mybir.AxisListType
ds = bass.ds

P = 128
B, S, D = 8, 1024, 256
T = B * S
H, HD = 16, 16
E, F = 8, 352
NS = 2
EA = E + NS
KD = D // P
FC = [128, 128, 96]
NBLK = T // P
TT = 512
TB = TT // P
NT = T // TT
MOE_TILES = 2 * T // P + E
EPS = 1e-5
ROUTE_SCALE = 2.5
GROUPS = B * H // 4
GH = 4
HQ = S // 2
NK = S // P
QR = 4 * HD
S1_ROWS = QR + 2
S2_ROWS = QR + 3


def hold(eng, sem, value, passed):
    eng.wait_ge(sem, value).then_inc(passed, 1)


class Chain:

    def __init__(self, eng, sem, base=0, passed=None):
        self.eng, self.sem, self.base, self.passed, self.k = eng, sem, base, passed, 0

    def link(self, ins):
        ins.then_inc(self.sem, 1)
        self.k += 1
        if self.passed is None:
            self.eng.wait_ge(self.sem, self.base + self.k)
        else:
            hold(self.eng, self.sem, self.base + self.k, self.passed)


def steps(eng, n, unroll, emit):
    turns = (n - 2) // unroll
    emit(0, 0, 0, True, n == 1)
    with eng.Fori(0, turns) as i:
        for u in range(unroll):
            emit(i * unroll + (1 + u), (1 + u) % unroll, i + (1 + u) // unroll, False, False)
    for j in range(1 + turns * unroll, n):
        emit(j, j % unroll, j // unroll, False, j == n - 1)


def build(nc, x, wqkv, gate_wt, w_gate, w_up, w_down, sw_gate, sw_up, sw_down, ident_in, tri_in, ali, out):
    with ExitStack() as kernel_ctx:
        def dram(name, shape, dt=F32):
            return nc.dram_tensor(name, shape, dt, kind="Internal").ap()

        scratch = dict(
            xn=dram("xn_scratch", [T, D]),
            qk=dram("qk_scratch", [2, 2 * D, T]),
            v=dram("v_scratch", [T, D]),
            lists=dram("lists_scratch", [E * T, 1], I32),
            ali=dram("ali_scratch", [H + 1, 2, S]),
            credit=dram("credit_scratch", [2, P, 1]),
            base=dram("base_scratch", [T, D]),
            yr=dram("yr_scratch", [MOE_TILES * P, D]),
        )

        def sb(name, shape, dt=F32):
            return kernel_ctx.enter_context(nc.sbuf_tensor(name, shape, dt))

        keep = dict(
            ctx=kernel_ctx,
            ident=sb("ident", [P, P]),
            logits=sb("logits", [P, NBLK * E]),
            pick=sb("pick", [P, 2, NBLK]),
            slot=sb("slot", [P, 2, NBLK]),
            count=sb("count", [P, E]),
            em8=sb("em8", [P, E]),
        )
        project(nc, keep, scratch, x, wqkv, gate_wt, ident_in, tri_in, ali)
        experts(nc, keep, scratch, x, w_gate, w_up, w_down, sw_gate, sw_up, sw_down)
        attend(nc, keep, scratch, out)


def stage(nc, ctx, keep):
    def sb(name, shape, dt=F32):
        return ctx.enter_context(nc.sbuf_tensor(name, shape, dt))

    def ps(name, shape, dt=F32):
        return ctx.enter_context(nc.psum_tensor(name, shape, dt))

    def sem(name):
        return keep["ctx"].enter_context(nc.semaphore(name))

    return sb, ps, sem


def project(nc, keep, scratch, x, wqkv, gate_wt, ident_in, tri_in, ali):
    with ExitStack() as ctx:
        sb, ps, sem = stage(nc, ctx, keep)
        ident, logits, pick, slot, count, em8 = (keep[k] for k in ("ident", "logits", "pick", "slot", "count", "em8"))
        w32 = sb("w32", [P, KD, 3 * D])
        w_hi, w_lo = sb("w_hi", [P, KD, 3 * D], F32R), sb("w_lo", [P, KD, 3 * D], F32R)
        g32 = sb("g32", [P, KD, E])
        g_hi, g_lo = sb("g_hi", [P, KD, E], F32R), sb("g_lo", [P, KD, E], F32R)
        tri, ones = sb("tri", [P, P]), sb("ones", [P, P])
        zeros = sb("zeros", [P, E * T // P], I32)
        x_sb = [sb(f"x{i}", [P, TB, D]) for i in range(2)]
        xn = [sb(f"xn{i}", [P, TB, D]) for i in range(2)]
        xt_hi = [sb(f"xt_hi{i}", [P, KD, TT], F32R) for i in range(2)]
        xt_lo = [sb(f"xt_lo{i}", [P, KD, TT], F32R) for i in range(2)]
        qk_out = [sb(f"qk_out{i}", [P, 2, 4, TT], F32R) for i in range(2)]
        v_out = [sb(f"v_out{i}", [P, TB, D]) for i in range(2)]
        stats, mv = sb("stats", [P, TB, 6]), sb("mv", [P, TB, 2])
        ve, root, newt, half = sb("ve", [P, TB]), sb("root", [P, TB]), sb("newt", [P, TB]), sb("half", [P, TB])
        lt, cmp_a, cmp_b = sb("lt", [P, TB, E]), sb("cmp_a", [P, TB, E]), sb("cmp_b", [P, TB, E])
        top, idx = sb("top", [P, TB]), sb("idx", [P, 2, TB])
        chosen, pos, run = sb("chosen", [P, 2, TB, E]), sb("pos", [P, TB, E]), sb("run", [P, TB + 1, E])
        both = sb("both", [P, TB, E])
        region = sb("region", [P, E])
        sl = sb("sl", [P, 2, TB])
        slot_i = sb("slot_i", [P, 2, TB], I32)
        token_all = sb("token_all", [P, NBLK], I32)
        token = sb("token", [P, TB], I32)

        p_xt = ps("p_xt", [P, KD, TT])
        p_qk = [ps(f"p_qk{i}", [P, TT]) for i in range(2)]
        p_v = ps("p_v", [P, TB, D])
        p_g = ps("p_g", [P, TT])

        names = ("w_in ali_st const_in iota_done x_in0 x_in1 ve_ready pow_ready xn_ready xt_ps xt_hi_ok xt_lo_ok "
                 "qk_ps qk_hi_ok qk_lo_ok v_ps v_ok g_ps g_read m_ready cnt_ps slot_ready tok_ok "
                 "passed xn_st0 xn_st1 qk_st0 qk_st1 v_st0 v_st1 scat zero_st dve_ln dve_sel dve_pro pool_pro")
        s = {n: sem("a_" + n) for n in names.split()}

        block = ctx.enter_context(nc.Block())

        @block.sync
        def _(sp):
            sp.dma_start(w32[:], wqkv.rearrange("(k p) n -> p k n", p=P)).then_inc(s["w_in"], 16)
            sp.dma_start(g32[:], gate_wt.rearrange("(k p) e -> p k e", p=P)).then_inc(s["w_in"], 16)
            sp.dma_start(ident[:], ident_in).then_inc(s["const_in"], 16)
            sp.dma_start(tri[:], tri_in).then_inc(s["const_in"], 16)
            sp.dma_start(scratch["ali"], ali).then_inc(s["ali_st"], 16)
            for i in range(2):
                sp.sem_inc(s[f"xn_st{i}"], 16)
                sp.sem_inc(s[f"qk_st{i}"], 16)
                sp.sem_inc(s[f"v_st{i}"], 16)
            xr = x.rearrange("(n b p) d -> n p b d", p=P, b=TB)
            xnr = scratch["xn"].rearrange("(n b p) d -> n p b d", p=P, b=TB)
            vr = scratch["v"].rearrange("(n b p) d -> n p b d", p=P, b=TB)

            def load(n, u):
                sp.dma_start(x_sb[u][:], xr[n]).then_inc(s[f"x_in{u}"], 16)

            load(0, 0)

            def tile(n, u, turn, first, last):
                if not last:
                    if not first:
                        sp.wait_ge(s["xn_ready"], n)
                    nn = 1 if first else n + 1
                    sp.dma_start(x_sb[1 - u][:], xr[ds(nn, 1)].rearrange("o p b d -> p (o b) d")
                                 if not isinstance(nn, int) else xr[nn]).then_inc(s[f"x_in{1 - u}"], 16)
                pick_n = (lambda a: a[n]) if isinstance(n, int) else (lambda a: a[ds(n, 1)].rearrange("o p b d -> p (o b) d"))
                sp.wait_ge(s["xn_ready"], n + 1)
                sp.dma_start(pick_n(xnr), xn[u][:]).then_inc(s[f"xn_st{u}"], 16)
                sp.wait_ge(s["qk_lo_ok"], 4 * n + 4)
                for hl in range(2):
                    sp.dma_start(scratch["qk"][hl].rearrange("(c p) t -> p c t", p=P)[:, :, ds(n * TT, TT)],
                                 qk_out[u][:, hl].bitcast(F32)).then_inc(s[f"qk_st{u}"], 16)
                sp.wait_ge(s["v_ok"], n + 1)
                sp.dma_start(pick_n(vr), v_out[u][:]).then_inc(s[f"v_st{u}"], 16)

            steps(sp, NT, 2, tile)
            for i in range(2):
                sp.wait_ge(s[f"xn_st{i}"], 16 * (NT // 2 + 1))
                sp.wait_ge(s[f"qk_st{i}"], 32 * (NT // 2) + 16)
                sp.wait_ge(s[f"v_st{i}"], 16 * (NT // 2 + 1))
            sp.wait_ge(s["scat"], 16 * 2 * NBLK)
            sp.wait_ge(s["ali_st"], 16)

        @block.gpsimd
        def _(pool):
            g = nc.gpsimd
            g.memset(ones[:], 1.0).then_inc(s["iota_done"], 1)
            g.memset(half[:], -0.5).then_inc(s["iota_done"], 1)
            g.iota(em8[:], [[1, E]], base=-E, channel_multiplier=0,
                   allow_small_or_imprecise_dtypes=True).then_inc(s["iota_done"], 1)
            g.iota(region[:], [[T, E]], base=0, channel_multiplier=0,
                   allow_small_or_imprecise_dtypes=True).then_inc(s["iota_done"], 1)
            g.iota(token_all[:], [[P, NBLK]], base=0, channel_multiplier=1).then_inc(s["iota_done"], 1)
            g.memset(zeros[:], 0).then_inc(s["pool_pro"], 1)
            pool.wait_ge(s["pool_pro"], 1)
            g.dma_start(scratch["lists"].rearrange("(p n) o -> p (n o)", p=P), zeros[:]).then_inc(s["zero_st"], 16)
            pool.wait_ge(s["iota_done"], 5)

            def power(n):
                hold(pool, s["ve_ready"], n + 1, s["passed"])
                g.tensor_tensor(root[:], ve[:], half[:], ALU.pow).then_inc(s["pow_ready"], 1)

            power(0)

            def tile(n, u, turn, first, last):
                if not last:
                    power(n + 1)
                if not first:
                    hold(pool, s["scat"], n * (16 * 2 * TB), s["passed"])
                g.tensor_copy(token[:], token_all[:, ds(n * TB, TB)]).then_inc(s["tok_ok"], 1)
                hold(pool, s["tok_ok"], n + 1, s["passed"])
                hold(pool, s["slot_ready"], n + 1, s["passed"])
                if first:
                    pool.wait_ge(s["zero_st"], 16)
                for c in range(2):
                    for b in range(TB):
                        g.indirect_dma_start(
                            scratch["lists"], bass.IndirectOffsetOnAxis(slot_i[:, c, b:b + 1], 0),
                            token[:, b:b + 1], None).then_inc(s["scat"], 16)

            steps(pool, NT, 2, tile)

        @block.vector
        def _(dve):
            v = nc.vector
            pro = Chain(dve, s["dve_pro"])
            dve.wait_ge(s["w_in"], 32)
            pro.link(v.tensor_copy(w_hi[:], w32[:]))
            pro.link(v.tensor_copy(g_hi[:], g32[:]))
            pro.link(v.tensor_tensor(w_lo[:], w32[:], w_hi[:].bitcast(F32), ALU.subtract))
            pro.link(v.tensor_tensor(g_lo[:], g32[:], g_hi[:].bitcast(F32), ALU.subtract))
            pro.link(v.memset(run[:], 0.0))
            dve.wait_ge(s["iota_done"], 5)

            LN_LINKS = 6

            def layernorm(n, u, turn):
                c = Chain(dve, s["dve_ln"], n * LN_LINKS, s["passed"])
                dve.wait_ge(s[f"x_in{u}"], 16 * (turn + 1))
                for b in range(TB):
                    last = v.bn_stats(stats[:, b], x_sb[u][:, b])
                c.link(last)
                for b in range(TB):
                    last = v.bn_aggr(mv[:, b], stats[:, b])
                c.link(last)
                v.tensor_scalar(ve[:], mv[:, :, 1], EPS, None, ALU.add).then_inc(s["ve_ready"], 1)
                dve.wait_ge(s["pow_ready"], n + 1)
                c.link(v.tensor_tensor(newt[:], root[:], root[:], ALU.mult))
                c.link(v.tensor_tensor(newt[:], newt[:], ve[:], ALU.mult))
                c.link(v.tensor_scalar(newt[:], newt[:], -0.5, 1.5, ALU.mult, ALU.add))
                c.link(v.tensor_tensor(newt[:], newt[:], root[:], ALU.mult))
                dve.wait_ge(s[f"xn_st{u}"], 16 * (turn + 1))
                for b in range(TB):
                    last = v.tensor_scalar(xn[u][:, b], x_sb[u][:, b], mv[:, b, 0:1], newt[:, b:b + 1],
                                           ALU.subtract, ALU.mult)
                last.then_inc(s["xn_ready"], 1)
                assert c.k == LN_LINKS

            layernorm(0, 0, 0)
            SEL_LINKS = 24

            def choose(n, u, first):
                c = Chain(dve, s["dve_sel"], n * SEL_LINKS)
                dve.wait_ge(s["g_ps"], n + 1)
                lp = p_g[:, 0:TB * E].rearrange("p (b e) -> p b e", b=TB)
                v.tensor_copy(logits[:, ds(n * TB * E, TB * E)], p_g[:, 0:TB * E])
                c.link(v.tensor_copy(lt[:], lp))
                em = em8[:, None, :].to_broadcast([P, TB, E])

                def pick_top(src, k):
                    c.link(v.tensor_reduce(top[:], src, AX.X, ALU.max))
                    c.link(v.tensor_tensor(cmp_a[:], src, top[:, :, None].to_broadcast([P, TB, E]), ALU.is_equal))
                    c.link(v.tensor_tensor(cmp_b[:], cmp_a[:], em, ALU.mult))
                    c.link(v.tensor_reduce(idx[:, k], cmp_b[:], AX.X, ALU.min))
                    c.link(v.tensor_tensor(chosen[:, k], em, idx[:, k, :, None].to_broadcast([P, TB, E]), ALU.is_equal))

                pick_top(lt[:], 0)
                c.link(v.scalar_tensor_tensor(lt[:], chosen[:, 0], -1e30, lt[:], ALU.mult, ALU.add))
                pick_top(lt[:], 1)
                v.tensor_copy(pick[:, :, ds(n * TB, TB)], idx[:])
                v.tensor_tensor(both[:], chosen[:, 0], chosen[:, 1], ALU.add).then_inc(s["m_ready"], 1)
                dve.wait_ge(s["cnt_ps"], n + 1)
                before = p_g[:, 64:64 + TB * E].rearrange("p (b e) -> p b e", b=TB)
                total = p_g[:, 128:128 + TB * E].rearrange("p (b e) -> p b e", b=TB)
                for b in range(TB):
                    c.link(v.tensor_tensor(run[:, b + 1], run[:, b], total[:, b], ALU.add))
                c.link(v.tensor_tensor(pos[:], before, run[:, 0:TB], ALU.add))
                c.link(v.tensor_copy(run[:, 0], run[:, TB]))
                c.link(v.tensor_tensor(pos[:], pos[:], region[:, None, :].to_broadcast([P, TB, E]), ALU.add))
                for k in range(2):
                    c.link(v.tensor_tensor(cmp_a[:], pos[:], chosen[:, k], ALU.mult))
                    c.link(v.tensor_reduce(sl[:, k], cmp_a[:], AX.X, ALU.add))
                v.tensor_copy(slot[:, :, ds(n * TB, TB)], sl[:])
                if not first:
                    dve.wait_ge(s["scat"], n * (16 * 2 * TB))
                c.link(v.tensor_copy(slot_i[:], sl[:]))
                v.tensor_copy(count[:], run[:, 0]).then_inc(s["slot_ready"], 1)
                assert c.k == SEL_LINKS

            def tile(n, u, turn, first, last):
                dve.wait_ge(s["xt_hi_ok"], n + 1)
                v.tensor_tensor(xt_lo[u][:], p_xt[:], xt_hi[u][:].bitcast(F32), ALU.subtract).then_inc(s["xt_lo_ok"], 1)
                if not last:
                    layernorm(n + 1, 1 - u, turn if u == 0 else turn + 1)
                for c in range(4):
                    dve.wait_ge(s["qk_hi_ok"], 4 * n + c + 1)
                    v.scalar_tensor_tensor(qk_out[u][:, 1, c], p_qk[c % 2][:], 1.0 if c < 2 else 1 / 16,
                                           qk_out[u][:, 0, c].bitcast(F32), ALU.mult,
                                           ALU.subtract).then_inc(s["qk_lo_ok"], 1)
                choose(n, u, first)

            steps(dve, NT, 2, tile)

        @block.scalar
        def _(act):
            a = nc.scalar

            def tile(n, u, turn, first, last):
                act.wait_ge(s["xt_ps"], n + 1)
                a.copy(xt_hi[u][:], p_xt[:]).then_inc(s["xt_hi_ok"], 1)
                act.wait_ge(s[f"qk_st{u}"], 32 * turn + 16)
                for c in range(4):
                    act.wait_ge(s["qk_ps"], 4 * n + c + 1)
                    a.mul(qk_out[u][:, 0, c], p_qk[c % 2][:], 1.0 if c < 2 else 1 / 16).then_inc(s["qk_hi_ok"], 1)
                act.wait_ge(s[f"v_st{u}"], 16 * (turn + 1))
                act.wait_ge(s["v_ps"], n + 1)
                a.copy(v_out[u][:], p_v[:]).then_inc(s["v_ok"], 1)

            steps(act, NT, 2, tile)

        @block.tensor
        def _(pe):
            t = nc.tensor
            pe.wait_ge(s["const_in"], 32)
            pe.wait_ge(s["iota_done"], 5)
            pe.wait_ge(s["dve_pro"], 4)

            def turn_x(n, u):
                pe.wait_ge(s["xn_ready"], n + 1)
                for b in range(TB):
                    for k in range(KD):
                        last = t.transpose(p_xt[:, k, b * P:(b + 1) * P], xn[u][:, b, k * P:(k + 1) * P], ident[:])
                last.then_inc(s["xt_ps"], 1)

            turn_x(0, 0)

            def products(dst, lhs, rhs):
                n = 0
                for k in range(KD):
                    for a, b in ((0, 0), (0, 1), (1, 0)):
                        last = t.matmul(dst, lhs[a](k), rhs[b](k), start=(n == 0), stop=(n == 3 * KD - 1))
                        n += 1
                return last

            def tile(n, u, turn, first, last):
                pe.wait_ge(s["xt_lo_ok"], n + 1)
                if not last:
                    turn_x(n + 1, 1 - u)
                for c in range(4):
                    if not (first and c < 2):
                        pe.wait_ge(s["qk_lo_ok"], 4 * n + c - 1)
                    products(p_qk[c % 2][:], [lambda k, w=w: w[:, k, c * P:(c + 1) * P] for w in (w_hi, w_lo)],
                             [lambda k, w=w: w[u][:, k] for w in (xt_hi, xt_lo)]).then_inc(s["qk_ps"], 1)
                xs = lambda b: [lambda k, w=w: w[u][:, k, b * P:(b + 1) * P] for w in (xt_hi, xt_lo)]
                if not first:
                    pe.wait_ge(s["slot_ready"], n)
                for b in range(TB):
                    ins = products(p_g[:, b * E:(b + 1) * E], xs(b), [lambda k, w=w: w[:, k] for w in (g_hi, g_lo)])
                ins.then_inc(s["g_ps"], 1)
                if not first:
                    pe.wait_ge(s["v_ok"], n)
                for b in range(TB):
                    ins = products(p_v[:, b], xs(b), [lambda k, w=w: w[:, k, 2 * D:3 * D] for w in (w_hi, w_lo)])
                ins.then_inc(s["v_ps"], 1)
                pe.wait_ge(s["m_ready"], n + 1)
                t.matmul(p_g[:, 64:64 + TB * E], tri[:], both[:].rearrange("p b e -> p (b e)"), start=True, stop=True)
                t.matmul(p_g[:, 128:128 + TB * E], ones[:], both[:].rearrange("p b e -> p (b e)"),
                         start=True, stop=True).then_inc(s["cnt_ps"], 1)

            steps(pe, NT, 2, tile)


def experts(nc, keep, scratch, x, w_gate, w_up, w_down, sw_gate, sw_up, sw_down):
    with ExitStack() as ctx:
        sb, ps, sem = stage(nc, ctx, keep)
        ident, count = keep["ident"], keep["count"]
        GU, DN = 2 * F, len(FC) * D
        wgu = [sb(f"wgu_{h}", [P, KD * EA * GU], F32R) for h in ("hi", "lo")]
        wdn = [sb(f"wdn_{h}", [P, EA * DN], F32R) for h in ("hi", "lo")]
        gu32 = sb("gu32", [P, KD, GU])
        dn32 = sb("dn32", [P, DN])
        XB = 4
        x_sb = [sb(f"xe{i}", [P, D]) for i in range(XB)]
        ids = [sb(f"ids{i}", [P, 1], I32) for i in range(XB)]
        xt = [[sb(f"xet_{h}{i}", [P, KD, P], F32R) for i in range(2)] for h in ("hi", "lo")]
        gated, h_sb = sb("gated", [P, F]), sb("h_sb", [P, F])
        ht = [[sb(f"ht_{h}{i}", [P, 3, P], F32R) for i in range(2)] for h in ("hi", "lo")]
        y_sb = [sb(f"y{i}", [P, D]) for i in range(XB)]
        tile_no = sb("tile_no", [1, MOE_TILES])
        t_exp, t_cmp, t_blk = sb("t_exp", [1, MOE_TILES]), sb("t_cmp", [1, MOE_TILES]), sb("t_blk", [1, MOE_TILES])
        w_off_i, blk_i = sb("w_off_i", [1, 2, MOE_TILES], I32), sb("blk_i", [1, MOE_TILES], I32)
        nt_i, nt_f = sb("nt_i", [P, E], I32), sb("nt_f", [P, E])
        base, end, one8 = sb("base", [P, E]), sb("end", [P, E]), sb("one8", [P, E])
        adj = sb("adj", [P, E])
        yslot = sb("yslot", [P, 2, NBLK])
        keep_slot, pick = keep["slot"], keep["pick"]

        p_x = ps("pe_x", [P, KD, P])
        p_gate, p_up = ps("p_gate", [P, 512]), ps("p_up", [P, 512])
        p_h, p_y = ps("pe_h", [P, 3, P]), ps("pe_y", [P, 512])

        names = ("passed gu_in split tab tiles_ready pool_pro")
        s = {n: sem("e_" + n) for n in names.split()}

        block = ctx.enter_context(nc.Block())

        def gu_at(half_, k, e_off, up, n=F):
            return wgu[half_][:, ds(e_off + (k * EA * GU + up * F), n)]

        order = [8, 9] + list(range(8))

        def stream(name, more):
            ns = (more + " x_in0 x_in1 x_in2 x_in3 xt_ps xt_hi xt_lo gu_ps gated h_ok "
                  "ht_ps ht_hi ht_lo y_ps y_free y_st0 y_st1 y_st2 y_st3")
            return {n: sem(f"{name}_{n}") for n in ns.split()}

        sh, rt = stream("sh", "r_in0 r_in1 r_in2 r_in3"), stream("rt", "id_in0 id_in1 id_in2 id_in3")

        def io(eng, q, n, src, dst, ids_of=None, residual=None):
            def load(j, u, free):
                if free is not None:
                    eng.wait_ge(q["xt_ps"], free)
                if ids_of is None:
                    eng.dma_start(x_sb[u][:], src[ds(j * P, P)]).then_inc(q[f"x_in{u}"], 16)
                else:
                    blk = eng.value_load(ids_of[0:1, ds(j, 1)], min_val=0, max_val=E * T // P - 1)
                    eng.dma_start(ids[u][:], src[ds(blk * P, P)]).then_inc(q[f"id_in{u}"], 16)

            for i in range(XB):
                eng.sem_inc(q[f"y_st{i}"], 16)
            for j in range(XB - 1):
                load(j, j, None)

            def load_residual(j, u, turn):
                eng.wait_ge(q[f"y_st{u}"], 16 * (turn + 1))
                eng.dma_start(y_sb[u][:], residual[ds(j * P, P)]).then_inc(q[f"r_in{u}"], 16)

            if residual is not None:
                load_residual(0, 0, 0)
                load_residual(1, 1, 0)

            def step(j, u, turn, first, last):
                if isinstance(j, int) and j > 4:
                    if j + XB - 1 < n:
                        load(j + XB - 1, (u + XB - 1) % XB, j)
                else:
                    load(j + XB - 1, (u + XB - 1) % XB, None if first else j)
                if residual is not None and not (isinstance(j, int) and j + 2 >= n):
                    load_residual(j + 2, (u + 2) % XB, turn + (u + 2) // XB)
                eng.wait_ge(q["y_free"], j + 2)
                eng.dma_start(dst[ds(j * P, P)], y_sb[u][:]).then_inc(q[f"y_st{u}"], 16)

            steps_tail(eng, n, XB, step)
            for i in range(XB):
                eng.wait_ge(q[f"y_st{i}"], 16 * (n // XB + 1))

        def steps_tail(eng, n, unroll, emit):
            turns = (n - unroll) // unroll
            emit(0, 0, 0, True, False)
            with eng.Fori(0, turns) as i:
                for u in range(unroll):
                    emit(i * unroll + (1 + u), (1 + u) % unroll, i + (1 + u) // unroll, False, False)
            for j in range(1 + turns * unroll, n):
                emit(j, j % unroll, j // unroll, False, j == n - 1)

        @block.gpsimd
        def _(pool):
            g = nc.gpsimd
            g.memset(one8[:], 1.0).then_inc(s["pool_pro"], 1)
            g.iota(tile_no[:], [[1, MOE_TILES]], base=0, channel_multiplier=0,
                   allow_small_or_imprecise_dtypes=True).then_inc(s["pool_pro"], 1)
            k = 0
            for n, e in enumerate(order):
                hold(pool, s["gu_in"], 64 * (n + 1), s["passed"])
                wg = [w[:].rearrange("p (k e f) -> p k e f", k=KD, e=EA)[:, :, e] for w in wgu]
                g.tensor_copy(wg[0], gu32[:]).then_inc(s["pool_pro"], 1)
                dv = [[w[0:r, e * DN + c0:e * DN + c1] for w in wdn] + [dn32[0:r, c0:c1]]
                      for r, c0, c1 in ((P, 0, 2 * D), (FC[2], 2 * D, 3 * D))]
                for hi, lo, src in dv:
                    g.tensor_copy(hi, src).then_inc(s["pool_pro"], 1)
                k += 3
                pool.wait_ge(s["pool_pro"], 2 + k)
                g.tensor_tensor(wg[1], gu32[:], wg[0].bitcast(F32), ALU.subtract).then_inc(s["pool_pro"], 1)
                for hi, lo, src in dv:
                    g.tensor_tensor(lo, src, hi.bitcast(F32), ALU.subtract).then_inc(s["pool_pro"], 1)
                k += 3
                pool.wait_ge(s["pool_pro"], 2 + k)
                pool.sem_inc(s["split"], 1)
            def step(j, u, turn, first, last):
                hold(pool, rt[f"id_in{u}"], 16 * (turn + 1), s["passed"])
                g.indirect_dma_start(x_sb[u][:], None, scratch["xn"],
                                     bass.IndirectOffsetOnAxis(ids[u][:], 0)).then_inc(rt[f"x_in{u}"], 16)
            steps(pool, MOE_TILES, XB, step)

        def pe_stream(pe, q, n, subs, offsets, tiles):
            t = nc.tensor

            def turn_x(j, u, turn):
                pe.wait_ge(q[f"x_in{u}"], 16 * (turn + 1))
                for k in range(KD):
                    last = t.transpose(p_x[:, k], x_sb[u][:, k * P:(k + 1) * P], ident[:])
                last.then_inc(q["xt_ps"], 1)

            def down(job, par, group, sub, off):
                pe.wait_ge(q["ht_lo"], job + 1)
                if sub == 0:
                    pe.wait_ge(q["y_free"], group + 1)
                i, all_ = 0, 3 * len(FC)
                for c, rows in enumerate(FC):
                    for a, b in ((0, 0), (0, 1), (1, 0)):
                        last = t.matmul(p_y[:, 0:D], ht[a][par][0:rows, c], wdn[b][0:rows, ds(off + c * D, D)],
                                        start=(i == 0 and sub == 0), stop=(i == all_ - 1 and sub == subs - 1))
                        i += 1
                if sub == subs - 1:
                    last.then_inc(q["y_ps"], 1)

            held = {}

            def step(j, u, turn, first, last):
                par = u % 2
                if first:
                    turn_x(0, 0, 0)
                offs = offsets(pe, j)
                prev = held.get("prev")
                pe.wait_ge(q["xt_lo"], j + 1)
                for sub in range(subs):
                    job = subs * j + sub
                    jp = job_parity(subs, par, sub)
                    gu_off, dn_off = offs[sub]
                    for up, dst in ((0, p_gate), (1, p_up)):
                        i = 0
                        for k in range(KD):
                            for a, b in ((0, 0), (0, 1), (1, 0)):
                                ins = t.matmul(dst[:, 0:F], xt[a][par][:, k], gu_at(b, k, gu_off, up),
                                               start=(i == 0), stop=(i == 3 * KD - 1))
                                i += 1
                    ins.then_inc(q["gu_ps"], 1)
                    if not (first and sub == 0):
                        if sub == 0:
                            down(job - 1, 1 - jp, j - 1, subs - 1, prev_off(pe, j, subs))
                        else:
                            down(job - 1, 1 - jp, j, sub - 1, offs[sub - 1][1])
                    if sub == 0 and not last:
                        turn_x(j + 1, (u + 1) % XB, turn + (1 if u == XB - 1 else 0))
                    pe.wait_ge(q["h_ok"], job + 1)
                    for c, rows in enumerate(FC):
                        ins = t.transpose(p_h[0:rows, c], h_sb[:, c * P:c * P + rows], ident[:])
                    ins.then_inc(q["ht_ps"], 1)
                if last:
                    down(subs * j + subs - 1, job_parity(subs, par, subs - 1), j, subs - 1, offs[subs - 1][1])

            def prev_off(pe, j, subs):
                return tiles(pe, j)

            steps(pe, n, XB, step)

        def job_parity(subs, par, sub):
            return par if subs == 1 else sub

        def act_stream(act, q, n, subs):
            a = nc.scalar

            def split_x(j, par):
                act.wait_ge(q["xt_ps"], j + 1)
                a.copy(xt[0][par][:], p_x[:]).then_inc(q["xt_hi"], 1)

            def step(j, u, turn, first, last):
                par = u % 2
                if first:
                    split_x(0, 0)
                for sub in range(subs):
                    job = subs * j + sub
                    act.wait_ge(q["gu_ps"], job + 1)
                    a.activation(gated[:], p_gate[:, 0:F], ACT.Silu).then_inc(q["gated"], 1)
                    if sub == 0 and not last:
                        split_x(j + 1, 1 - par)
                    act.wait_ge(q["ht_ps"], job + 1)
                    jp = job_parity(subs, par, sub)
                    a.copy(ht[0][jp][:, 0:2], p_h[:, 0:2])
                    a.copy(ht[0][jp][0:FC[2], 2], p_h[0:FC[2], 2]).then_inc(q["ht_hi"], 1)

            steps(act, n, XB, step)

        def dve_stream(dve, q, n, subs):
            v = nc.vector

            def split_x(j, par):
                dve.wait_ge(q["xt_hi"], j + 1)
                v.tensor_tensor(xt[1][par][:], p_x[:], xt[0][par][:].bitcast(F32), ALU.subtract).then_inc(q["xt_lo"], 1)

            def finish(j, u, turn):
                dve.wait_ge(q["y_ps"], j + 1)
                if subs == NS:
                    dve.wait_ge(q[f"r_in{u}"], 16 * (turn + 1))
                    v.tensor_tensor(y_sb[u][:], p_y[:, 0:D], y_sb[u][:], ALU.add).then_inc(q["y_free"], 1)
                else:
                    dve.wait_ge(q[f"y_st{u}"], 16 * (turn + 1))
                    v.tensor_copy(y_sb[u][:], p_y[:, 0:D]).then_inc(q["y_free"], 1)

            dve.sem_inc(q["y_free"], 1)

            def step(j, u, turn, first, last):
                par = u % 2
                if first:
                    split_x(0, 0)
                for sub in range(subs):
                    job = subs * j + sub
                    dve.wait_ge(q["gated"], job + 1)
                    v.tensor_tensor(h_sb[:], p_up[:, 0:F], gated[:], ALU.mult).then_inc(q["h_ok"], 1)
                    if sub == 0 and not first:
                        finish(j - 1, (u - 1) % XB, turn - (1 if u == 0 else 0))
                    if sub == 0 and not last:
                        split_x(j + 1, 1 - par)
                    dve.wait_ge(q["ht_hi"], job + 1)
                    jp = job_parity(subs, par, sub)
                    v.tensor_tensor(ht[1][jp][:, 0:2], p_h[:, 0:2], ht[0][jp][:, 0:2].bitcast(F32), ALU.subtract)
                    v.tensor_tensor(ht[1][jp][0:FC[2], 2], p_h[0:FC[2], 2], ht[0][jp][0:FC[2], 2].bitcast(F32),
                                    ALU.subtract).then_inc(q["ht_lo"], 1)
                if last:
                    finish(j, u, turn)

            steps(dve, n, XB, step)

        @block.sync
        def _(sp):
            for n, e in enumerate(order):
                if n:
                    sp.wait_ge(s["split"], n)
                if e < E:
                    g, u, d = w_gate[e], w_up[e], w_down[e]
                else:
                    cols = slice((e - E) * F, (e - E + 1) * F)
                    g, u, d = sw_gate[:, cols], sw_up[:, cols], sw_down[cols]
                sp.dma_start(gu32[:, :, 0:F], g.rearrange("(k p) f -> p k f", p=P)).then_inc(s["gu_in"], 16)
                sp.dma_start(gu32[:, :, F:2 * F], u.rearrange("(k p) f -> p k f", p=P)).then_inc(s["gu_in"], 16)
                sp.dma_start(dn32[:, 0:2 * D].rearrange("p (c d) -> p c d", c=2),
                             d[0:2 * P].rearrange("(c p) d -> p c d", p=P)).then_inc(s["gu_in"], 16)
                sp.dma_start(dn32[0:FC[2], 2 * D:3 * D], d[2 * P:F]).then_inc(s["gu_in"], 16)
            io(sp, sh, NBLK, scratch["xn"], scratch["base"], None, x)
            sp.wait_ge(s["tiles_ready"], 1)
            io(sp, rt, MOE_TILES, scratch["lists"], scratch["yr"], blk_i)

        @block.vector
        def _(dve):
            v = nc.vector
            c = Chain(dve, s["tab"])
            dve.wait_ge(s["pool_pro"], 2)
            c.link(v.tensor_scalar(nt_f[:], count[:], float(P - 1), None, ALU.add))
            c.link(v.tensor_copy(nt_i[:], nt_f[:]))
            c.link(v.tensor_scalar(nt_i[:], nt_i[:], 7, None, ALU.arith_shift_right))
            c.link(v.tensor_copy(nt_f[:], nt_i[:]))
            c.link(v.tensor_tensor_scan(end[:], one8[:], nt_f[:], 0.0, ALU.mult, ALU.add))
            c.link(v.tensor_tensor(base[:], end[:], nt_f[:], ALU.subtract))
            c.link(v.tensor_scalar(t_exp[:], tile_no[:], end[0:1, 0:1], None, ALU.is_ge))
            for e in range(1, E - 1):
                c.link(v.scalar_tensor_tensor(t_exp[:], tile_no[:], end[0:1, e:e + 1], t_exp[:], ALU.is_ge, ALU.add))
            c.link(v.tensor_copy(t_blk[:], tile_no[:]))
            for e in range(E):
                c.link(v.tensor_scalar(adj[:, e:e + 1], base[:, e:e + 1], -1.0, float(e * T // P), ALU.mult, ALU.add))
                c.link(v.tensor_scalar(t_cmp[:], t_exp[:], float(e), adj[0:1, e:e + 1], ALU.is_equal, ALU.mult))
                c.link(v.tensor_tensor(t_blk[:], t_blk[:], t_cmp[:], ALU.add))
            c.link(v.tensor_scalar(blk_i[:], t_blk[:], float(E * T // P - 1), None, ALU.min))
            c.link(v.tensor_scalar(w_off_i[:, 0], t_exp[:], float(GU), None, ALU.mult))
            c.link(v.tensor_scalar(w_off_i[:, 1], t_exp[:], float(DN), None, ALU.mult))
            c.link(v.tensor_copy(yslot[:], keep_slot[:]))
            for e in range(E):
                c.link(v.tensor_scalar(base[:, e:e + 1], adj[:, e:e + 1], float(-P), None, ALU.mult))
                for k in range(2):
                    c.link(v.tensor_scalar(keep_slot[:, k], pick[:, k], float(e - E), base[:, e:e + 1],
                                           ALU.is_equal, ALU.mult))
                    c.link(v.tensor_tensor(yslot[:, k], yslot[:, k], keep_slot[:, k], ALU.add))
            v.tensor_copy(keep_slot[:], yslot[:]).then_inc(s["tiles_ready"], 1)
            dve_stream(dve, sh, NBLK, NS)
            dve_stream(dve, rt, MOE_TILES, 1)

        @block.scalar
        def _(act):
            act_stream(act, sh, NBLK, NS)
            act_stream(act, rt, MOE_TILES, 1)

        @block.tensor
        def _(pe):
            pe.wait_ge(s["split"], NS)
            shared = [((E + i) * GU, (E + i) * DN) for i in range(NS)]
            pe_stream(pe, sh, NBLK, NS, lambda pe, j: shared, lambda pe, j: shared[-1][1])
            pe.wait_ge(s["split"], EA)
            pe.wait_ge(s["tiles_ready"], 1)

            def offsets(pe, j):
                gu = pe.value_load(w_off_i[0:1, 0, ds(j, 1)], min_val=0, max_val=(E - 1) * GU)
                dn = pe.value_load(w_off_i[0:1, 1, ds(j, 1)], min_val=0, max_val=(E - 1) * DN)
                return [(gu, dn)]

            def before(pe, j):
                return pe.value_load(w_off_i[0:1, 1, ds(j - 1, 1)], min_val=0, max_val=(E - 1) * DN)

            pe_stream(pe, rt, MOE_TILES, 1, offsets, before)


def attend(nc, keep, scratch, out):
    with ExitStack() as ctx:
        sb, ps, sem = stage(nc, ctx, keep)
        ident, logits, pick, slot, em8 = (keep[k] for k in ("ident", "logits", "pick", "slot", "em8"))
        NB_OP = 3
        k_op = [sb(f"k_op{i}", [S2_ROWS, GH, S], F32R) for i in range(NB_OP)]
        q_op = [sb(f"q_op{i}", [96, GH, S], F32R) for i in range(NB_OP)]
        v_in = [sb(f"v_in{i}", [P, NK, GH * HD]) for i in range(NB_OP)]
        v_op = [sb(f"v_op{i}", [P, NK, GH, 32]) for i in range(NB_OP)]
        probs = [sb(f"probs{i}", [P, GH, HQ]) for i in range(4)]
        mx = [sb(f"mx{i}", [P, 4, 2]) for i in range(2)]
        neg = [sb(f"neg{i}", [P, 4], F32R) for i in range(2)]
        m_row = [sb(f"m_row{i}", [4, P], F32R) for i in range(4)]
        o_sb = [sb(f"o_sb{i}", [P, HQ]) for i in range(2)]
        rec = sb("rec", [P, 4, GH])
        att = sb("att", [P, 2 * NK, D])
        base_c = [sb(f"base_c{i}", [P, D]) for i in range(2)]
        y_c = [[sb(f"y_c{k}{i}", [P, D]) for i in range(2)] for k in range(2)]
        fin = sb("fin", [P, 3, NK, D])
        slot_i = sb("yslot_i", [P, 2, NBLK], I32)
        col_i = [sb(f"col_i{i}", [P, 2], I32) for i in range(2)]
        col_w = [sb(f"col_w{i}", [P, 2]) for i in range(2)]
        wts = sb("wts", [P, 2, NBLK])
        ex, cmp_ = (fin[:, 0, 2 * i:2 * i + 2].rearrange("p q d -> p (q d)").rearrange("p (n e) -> p n e", e=E)
                    for i in range(2))
        t64, z64 = sb("t64", [P, NBLK]), sb("z64", [P, NBLK])

        p1 = [ps(f"p1_{i}", [P, 512]) for i in range(3)]
        p2 = [ps(f"p2_{i}", [P, 512]) for i in range(3)]
        p_o = [ps(f"p_o{i}", [P, HQ]) for i in range(2)]

        names = ("passed ones_in init s1_ps s1_read s2_ps s2_read neg_ok m_ok pv_done v_ok o_ok rec_ok att_ok sub_ok "
                 "ex_ok w_ready dve_w pool_c col_ok o_st0 o_st1 c_ok base_in0 base_in1 yg_in0 yg_in1 fin_base fin_y "
                 "dve_f fin_ok fin_st")
        s = {n: sem("t_" + n) for n in names.split()}
        k_in = [sem(f"t_k_in{u}") for u in range(NB_OP)]
        v_in_s = [sem(f"t_v_in{u}") for u in range(NB_OP)]
        m_in = [sem(f"t_m_in{c}") for c in range(4)]

        UNITS = 2 * NK * GH
        HALF = UNITS // 2
        MAX_UNITS = 2 * GH * 4 * 2
        CHUNK = 8
        CHUNKS = MAX_UNITS // CHUNK
        AHEAD = [min(MAX_UNITS, MAX_UNITS * (n + 1) // (UNITS - 3)) for n in range(UNITS)]
        TURN_AT = {CHUNK * c + 10: c for c in range(CHUNKS - 1)} | {UNITS - 1: CHUNKS - 1}
        OUT_COPY, OUT_TURN = 6, 12
        V_SPREAD = 20
        R1 = MAX_UNITS + 2
        R2 = UNITS + CHUNKS

        def ring1(g, first):
            return MAX_UNITS if first else g * R1 + (MAX_UNITS - 1)

        def bank1(first, r):
            return ((MAX_UNITS if first else MAX_UNITS - 1) + r) % 3

        def ring2(g):
            return g * R2 + CHUNKS

        def bank2(r):
            return (CHUNKS + r) % 3

        assert R1 % 3 == 0 and R2 % 3 == 0

        def groups(eng, emit):
            turns = (GROUPS - 2) // 3
            assert turns * 3 == GROUPS - 2
            emit(0, 0, 0, False, True)
            with eng.Fori(0, turns) as i:
                for r in range(3):
                    emit(i * 3 + (1 + r), (1 + r) % 3, i + (1 + r) // 3, True, True)
            emit(GROUPS - 1, (GROUPS - 1) % 3, (GROUPS - 1) // 3, True, False)

        def following(u, turn):
            return (u + 1) % 3, turn + (1 if u == 2 else 0)

        block = ctx.enter_context(nc.Block())

        @block.sync
        def _(sp):
            qk, ali = scratch["qk"], scratch["ali"]
            sp.wait_ge(s["init"], 2 * NB_OP)
            for i in range(NB_OP):
                sp.dma_start(k_op[i][QR + 2:QR + 3].bitcast(F32),
                             ali[H:H + 1, 0:1].to_broadcast([1, GH, S])).then_inc(s["ones_in"], 16)

            def load(g, u):
                b, hg = g // (H // GH), g % (H // GH)
                for base, op, parts in ((0, k_op, (0, 1, 0, 1)), (D, q_op, (0, 0, 1, 1))):
                    for r, hl in enumerate(parts):
                        sp.dma_start(op[u][r * HD:(r + 1) * HD].bitcast(F32),
                                     qk[hl][ds(hg * (GH * HD) + base, GH * HD), ds(b * S, S)]
                                     .rearrange("(h d) t -> d h t", d=HD)).then_inc(k_in[u], 16)
                sp.dma_start(k_op[u][QR:QR + 2].bitcast(F32),
                             ali[ds(hg * GH, GH)].rearrange("h a t -> a h t")).then_inc(k_in[u], 16)
                sp.dma_start(v_in[u][:], scratch["v"][ds(b * S, S), ds(hg * (GH * HD), GH * HD)]
                             .rearrange("(k p) c -> p k c", p=P)).then_inc(v_in_s[u], 16)

            def send_max(g, u):
                for c in range(CHUNKS):
                    half, h = divmod(c, GH)
                    sp.wait_ge(s["m_ok"], g * CHUNKS + (c + 1))
                    sp.dma_start(q_op[u][QR + 2:QR + 3, h, half * HQ:(half + 1) * HQ]
                                 .rearrange("o (q c) -> o q c", q=4).bitcast(F32),
                                 m_row[c % 4][:].bitcast(F32)).then_inc(m_in[c % 4], 16)

            load(0, 0)
            load(1, 1)
            send_max(0, 0)

            def group(g, u, turn, has_prev, has_next):
                if has_next and not (isinstance(g, int) and g + 2 >= GROUPS):
                    if has_prev:
                        sp.wait_ge(s["pv_done"], g * (2 * NK) + NK)
                    load((g + 2) % GROUPS, (u + 2) % 3)
                if has_next:
                    send_max(g + 1, following(u, turn)[0])

            groups(sp, group)
            for i in range(NB_OP):
                n_loads = len([g for g in range(GROUPS + 1) if g % 3 == i])
                sp.wait_ge(k_in[i], n_loads * 16 * 9)
                sp.wait_ge(v_in_s[i], n_loads * 16)
            for half in range(2):
                sp.wait_ge(s["fin_ok"], half + 1)
                ring = (B - 1) % 2 * NK + 4 * half
                rows = ((B - 1) * NK + 4 * half) * P
                sp.dma_start(out[rows:rows + 4 * P].rearrange("(q p) d -> p q d", p=P),
                             att[:, ring:ring + 4]).then_inc(s["fin_st"], 16)
            sp.wait_ge(s["fin_st"], 32)

        @block.gpsimd
        def _(pool):
            g_ = nc.gpsimd
            for i in range(NB_OP):
                g_.memset(q_op[i][QR:96].bitcast(F32), 1.0).then_inc(s["init"], 1)
                pool.wait_ge(s["init"], 2 * i + 1)
                g_.memset(v_op[i][:], 1.0).then_inc(s["init"], 1)
                pool.wait_ge(s["init"], 2 * i + 2)
            g_.tensor_copy(slot_i[:], slot[:]).then_inc(s["pool_c"], 1)
            pool.wait_ge(s["pool_c"], 1)
            pool.wait_ge(s["w_ready"], 1)
            for i in range(2):
                pool.dma_start(scratch["credit"][i], wts[:, 0, 0:1]).then_inc(s[f"o_st{i}"], 16)

            CPB = 7

            def combine(n, u, turn, ring):
                c = Chain(pool, s["pool_c"], n * CPB + 1, s["passed"])
                pool.dma_start(base_c[u][:], scratch["base"][ds(n * P, P)]).then_inc(s[f"base_in{u}"], 16)
                c.link(g_.tensor_copy(col_w[u][:], wts[:, :, ds(n, 1)].rearrange("p a o -> p (a o)")))
                c.link(g_.tensor_copy(col_i[u][:], slot_i[:, :, ds(n, 1)].rearrange("p a o -> p (a o)")))
                for k in range(2):
                    g_.indirect_dma_start(y_c[k][u][:], None, scratch["yr"],
                                          bass.IndirectOffsetOnAxis(col_i[u][:, k:k + 1], 0)).then_inc(s[f"yg_in{u}"], 16)
                hold(pool, s[f"base_in{u}"], 16 * (turn + 1), s["passed"])
                hold(pool, s[f"o_st{u}"], 16 * (turn + 1), s["passed"])
                acc = base_c[u]
                c.link(g_.tensor_tensor(acc[:], acc[:], att[:, ds(ring, 1)].rearrange("p o d -> p (o d)"), ALU.add))
                hold(pool, s[f"yg_in{u}"], 32 * (turn + 1), s["passed"])
                for k in range(2):
                    y = y_c[k][u]
                    c.link(g_.tensor_scalar(y[:], y[:], col_w[u][:, k:k + 1], None, ALU.mult))
                    c.link(g_.tensor_tensor(acc[:], acc[:], y[:], ALU.add))
                assert c.k == CPB
                pool.sem_inc(s["c_ok"], 1)
                pool.dma_start(out[ds(n * P, P)], acc[:]).then_inc(s[f"o_st{u}"], 16)

            GB = H // GH
            with pool.Fori(0, B - 1) as b:
                hold(pool, s["att_ok"], b * (GB * 2) + GB * 2, s["passed"])
                with pool.Fori(0, NK // 2) as i:
                    for u in range(2):
                        combine(b * NK + i * 2 + u, u, b * (NK // 2) + i, (b % 2) * NK + i * 2 + u)
            first = (B - 1) * NK
            pool.dma_start(fin[:, 0], scratch["base"][first * P:].rearrange("(q p) d -> p q d", p=P)).then_inc(s["fin_base"], 16)
            for q in range(NK):
                for k in range(2):
                    g_.indirect_dma_start(fin[:, 1 + k, q], None, scratch["yr"],
                                          bass.IndirectOffsetOnAxis(slot_i[:, k, first + q:first + q + 1], 0)
                                          ).then_inc(s["fin_y"], 16)
            for i in range(2):
                pool.wait_ge(s[f"o_st{i}"], 16 * ((B - 1) * NK // 2 + 1))

        @block.vector
        def _(dve):
            v = nc.vector
            c = Chain(dve, s["dve_w"])
            lg = logits[:].rearrange("p (n e) -> p n e", e=E)
            wide = lambda a: a[:, :, None].to_broadcast([P, NBLK, E])
            c.link(v.tensor_reduce(t64[:], lg, AX.X, ALU.max))
            v.tensor_tensor(ex[:], lg, wide(t64), ALU.subtract).then_inc(s["sub_ok"], 1)

            def weights():
                dve.wait_ge(s["ex_ok"], 1)
                c.link(v.tensor_reduce(z64[:], ex[:], AX.X, ALU.add))
                c.link(v.reciprocal(t64[:], z64[:]))
                c.link(v.tensor_tensor(ex[:], ex[:], wide(t64), ALU.mult))
                em = em8[:, None, :].to_broadcast([P, NBLK, E])
                for k in range(2):
                    c.link(v.tensor_tensor(cmp_[:], em, wide(pick[:, k]), ALU.is_equal))
                    c.link(v.tensor_tensor(cmp_[:], cmp_[:], ex[:], ALU.mult))
                    c.link(v.tensor_reduce(wts[:, k], cmp_[:], AX.X, ALU.add))
                c.link(v.tensor_tensor(t64[:], wts[:, 0], wts[:, 1], ALU.add))
                c.link(v.tensor_scalar(t64[:], t64[:], 1e-20, None, ALU.add))
                c.link(v.reciprocal(z64[:], t64[:]))
                for k in range(2):
                    ins = v.scalar_tensor_tensor(wts[:, k], wts[:, k], ROUTE_SCALE, z64[:], ALU.mult, ALU.mult)
                ins.then_inc(s["w_ready"], 1)

            dve.sem_inc(s["c_ok"], 2 * NK)
            dve.sem_inc(s["s1_read"], 3)

            def max_unit(g, use, bank, w):
                dve.wait_ge(s["s1_ps"], use + 1)
                r = w % CHUNK
                m = mx[w // CHUNK % 2]
                v.tensor_reduce(m[:, r // 2, r % 2:r % 2 + 1], p1[bank][:], AX.X, ALU.max).then_inc(s["s1_read"], 1)
                if r == CHUNK - 1:
                    dve.wait_ge(s["s1_read"], use + 4)
                    v.tensor_reduce(neg[w // CHUNK % 2][:], m[:], AX.X, ALU.max, negate=True).then_inc(s["neg_ok"], 1)

            def output(g, half, use, bank):
                x_no = g * 2 + half
                b, hg = g // (H // GH), g % (H // GH)
                dve.wait_ge(s["s1_ps"], use + 1)
                ot = p1[bank][:].rearrange("p (q h c) -> p q h c", q=4, h=GH)
                v.reciprocal(rec[:], ot[:, :, :, HD]).then_inc(s["rec_ok"], 1)
                dve.wait_ge(s["c_ok"], b * NK + NK)
                dve.wait_ge(s["rec_ok"], x_no + 1)
                dst = att[:, ds((b % 2) * NK + 4 * half, 4), ds(hg * (GH * HD), GH * HD)]
                v.tensor_tensor(dst.rearrange("p q (h c) -> p q h c", h=GH), ot[:, :, :, 0:HD],
                                rec[:, :, :, None].to_broadcast([P, 4, GH, HD]), ALU.mult).then_inc(s["att_ok"], 1)
                dve.wait_ge(s["att_ok"], x_no + 1)
                dve.sem_inc(s["s1_read"], 1)

            FIN_LINKS = 3 * 4

            def final(half):
                cf = Chain(dve, s["dve_f"], half * FIN_LINKS)
                dve.wait_ge(s["fin_base"], 16)
                dve.wait_ge(s["fin_y"], 16 * 2 * NK)
                ring = (B - 1) % 2 * NK + 4 * half
                for step in range(3):
                    for q in range(4):
                        acc = att[:, ring + q]
                        n = (B - 1) * NK + 4 * half + q
                        if step == 0:
                            cf.link(v.tensor_tensor(acc, acc, fin[:, 0, 4 * half + q], ALU.add))
                        else:
                            cf.link(v.scalar_tensor_tensor(acc, fin[:, step, 4 * half + q], wts[:, step - 1, n:n + 1],
                                                           acc, ALU.mult, ALU.add))
                dve.sem_inc(s["fin_ok"], 1)

            for w in range(MAX_UNITS):
                max_unit(0, w, w % 3, w)
            weights()

            def group(g, u, turn, has_prev, has_next):
                base, r, w = ring1(g, not has_prev), 0, 0
                for n in range(UNITS):
                    if has_next:
                        while w < AHEAD[n]:
                            max_unit(g + 1, base + r, bank1(not has_prev, r), w)
                            w, r = w + 1, r + 1
                    if n % HALF == OUT_TURN and (n >= HALF or has_prev):
                        pg, ph = (g, 0) if n >= HALF else (g - 1, 1)
                        output(pg, ph, base + r, bank1(not has_prev, r))
                        r += 1
                if not has_next:
                    final(0)
                    output(g, 1, base + r, bank1(not has_prev, r))
                    final(1)

            groups(dve, group)

        @block.scalar
        def _(act):
            a = nc.scalar
            act.wait_ge(s["sub_ok"], 1)
            a.activation(ex[:], ex[:], ACT.Exp).then_inc(s["ex_ok"], 1)
            act.sem_inc(s["s2_read"], 3)
            act.sem_inc(s["o_ok"], 2)
            act.sem_inc(s["pv_done"], NK)

            def row_copy(g, use, bank, c):
                act.wait_ge(s["s2_ps"], use + 1)
                if c >= 4 or not (isinstance(g, int) and g == 0):
                    act.wait_ge(m_in[c % 4], g * 32 + 16 * (c // 4))
                a.copy(m_row[c % 4][:], p2[bank][0:4, 0:P]).then_inc(s["s2_read"], 1)
                act.wait_ge(s["s2_read"], use + 4)
                act.sem_inc(s["m_ok"], 1)

            def spread_v(g, u, turn):
                act.wait_ge(v_in_s[u], 16 * (turn + 1))
                a.copy(v_op[u][:, :, :, 0:HD], v_in[u][:].rearrange("p k (h d) -> p k h d", h=GH)).then_inc(s["v_ok"], 1)

            def output_copy(g, half):
                act.wait_ge(s["pv_done"], (g * 2 + half) * NK + 2 * NK)
                a.copy(o_sb[half][:], p_o[half][:]).then_inc(s["o_ok"], 1)

            act.wait_ge(s["init"], 2 * NB_OP)
            spread_v(0, 0, 0)
            for c in range(CHUNKS):
                row_copy(0, c, c % 3, c)

            def group(g, u, turn, has_prev, has_next):
                base, r = ring2(g), 0
                nu, nt = following(u, turn)
                for n in range(UNITS):
                    half, kb, h = n // HALF, n % HALF // GH, n % GH
                    act.wait_ge(s["s2_ps"], base + (r + 1))
                    if h == 0:
                        act.wait_ge(s["pv_done"], g * (2 * NK) + (half * NK + kb - 3 + NK))
                    a.activation(probs[kb % 4][:, h], p2[bank2(r)][:], ACT.Exp).then_inc(s["s2_read"], 1)
                    r += 1
                    if n in TURN_AT and has_next:
                        row_copy(g + 1, base + r, bank2(r), TURN_AT[n])
                        r += 1
                    if n % HALF == OUT_COPY and (n >= HALF or has_prev):
                        output_copy(*((g, 0) if n >= HALF else (g - 1, 1)))
                    if n == V_SPREAD and has_next:
                        spread_v(g + 1, nu, nt)
                if not has_next:
                    output_copy(g, 1)

            groups(act, group)

        @block.tensor
        def _(pe):
            t = nc.tensor

            def max_unit(u, use, bank, w):
                chunk, r = divmod(w, CHUNK)
                half, h = divmod(chunk, GH)
                qb, kh = 4 * half + r // 2, r % 2
                pe.wait_ge(s["s1_read"], use + 1)
                t.matmul(p1[bank][:], q_op[u][0:S1_ROWS, h, qb * P:(qb + 1) * P],
                         k_op[u][0:S1_ROWS, h, kh * 512:(kh + 1) * 512], start=True, stop=True).then_inc(s["s1_ps"], 1)

            def turn_max(g, use, bank, c):
                pe.wait_ge(s["neg_ok"], g * CHUNKS + (c + 1))
                pe.wait_ge(s["s2_read"], use + 1)
                t.transpose(p2[bank][0:4, 0:P], neg[c % 2][:].bitcast(F32), ident[:]).then_inc(s["s2_ps"], 1)

            def score_unit(g, u, use, bank, n):
                half, kb, h = n // HALF, n % HALF // GH, n % GH
                pe.wait_ge(s["s2_read"], use + 1)
                if kb == 0:
                    pe.wait_ge(m_in[h], g * 32 + 16 * (half + 1))
                t.matmul(p2[bank][:], k_op[u][0:S2_ROWS, h, kb * P:(kb + 1) * P],
                         q_op[u][0:S2_ROWS, h, half * HQ:(half + 1) * HQ], start=True, stop=True).then_inc(s["s2_ps"], 1)

            def products(g, u, half, kb, read):
                pe.wait_ge(s["s2_read"], read)
                if kb == 0:
                    pe.wait_ge(s["v_ok"], g + 1)
                    pe.wait_ge(s["o_ok"], g * 2 + (half + 1))
                for h in range(GH):
                    ins = t.matmul(p_o[half][32 * h:32 * h + 32], v_op[u][:, kb, h], probs[kb % 4][:, h],
                                   start=(kb == 0), stop=(kb == NK - 1))
                ins.then_inc(s["pv_done"], 1)

            def turn_output(g, half, use, bank):
                pe.wait_ge(s["o_ok"], g * 2 + (half + 3))
                pe.wait_ge(s["s1_read"], use + 1)
                for q in range(4):
                    ins = t.transpose(p1[bank][:, q * P:(q + 1) * P], o_sb[half][:, q * P:(q + 1) * P], ident[:])
                ins.then_inc(s["s1_ps"], 1)

            pe.wait_ge(s["ones_in"], 16 * NB_OP)
            pe.wait_ge(k_in[0], 16 * 9)
            for w in range(MAX_UNITS):
                max_unit(0, w, w % 3, w)
                if w % CHUNK == 2 and w >= CHUNK:
                    turn_max(0, w // CHUNK - 1, (w // CHUNK - 1) % 3, w // CHUNK - 1)
            turn_max(0, CHUNKS - 1, (CHUNKS - 1) % 3, CHUNKS - 1)

            def group(g, u, turn, has_prev, has_next):
                b1, r1, w = ring1(g, not has_prev), 0, 0
                b2, r2 = ring2(g), 0
                nu, nt = following(u, turn)
                read = {}
                for n in range(UNITS):
                    score_unit(g, u, b2 + r2, bank2(r2), n)
                    read[n] = b2 + (r2 + 4)
                    r2 += 1
                    if has_next:
                        if n == 0:
                            pe.wait_ge(k_in[nu], (nt + 1) * (16 * 9))
                        while w < AHEAD[n]:
                            max_unit(nu, b1 + r1, bank1(not has_prev, r1), w)
                            w, r1 = w + 1, r1 + 1
                        if n in TURN_AT:
                            turn_max(g + 1, b2 + r2, bank2(r2), TURN_AT[n])
                            r2 += 1
                    half, l = divmod(n, HALF)
                    if l == 2 and half == 0 and has_prev:
                        products(g - 1, (u + 2) % 3, 1, NK - 1, b2 + 2)
                    elif l % GH == 2 and n != 2:
                        kb = l // GH - 1
                        if kb >= 0:
                            products(g, u, half, kb, read[n - 3])
                        else:
                            products(g, u, 0, NK - 1, read[n - 3])
                    if l == OUT_TURN and (half or has_prev):
                        turn_output(*((g, 0) if half else (g - 1, 1)), b1 + r1, bank1(not has_prev, r1))
                        r1 += 1
                if not has_next:
                    products(g, u, 1, NK - 1, read[UNITS - 1])
                    turn_output(g, 1, b1 + r1, bank1(not has_prev, r1))

            groups(pe, group)


def kernel(L0_attn_x, L0_attn_W_kqv, L0_ffn_gate_w, L0_ffn_w_gate, L0_ffn_w_up, L0_ffn_w_down,
           L0_ffn_sw_gate, L0_ffn_sw_up, L0_ffn_sw_down):
    import concourse.bacc as bacc
    from concourse.bass_utils import run_bass_kernel_spmd

    f32 = np.float32
    ratio = (2 ** 8) ** (1.0 / H)
    slopes = np.array([1.0 / ratio ** (i + 1) for i in range(H)], dtype=f32)
    bias = slopes[:, None] * (np.arange(S) - (S - 1)).astype(f32)[None, :]
    top = (bias.view(np.uint32) & np.uint32(0xFFFFF000)).view(f32)
    ali = np.zeros((H + 1, 2, S), f32)
    ali[:H, 0], ali[:H, 1], ali[H] = top, bias - top, 1.0
    arrays = {
        "x": np.ascontiguousarray(L0_attn_x).reshape(T, D),
        "wqkv": np.ascontiguousarray(np.asarray(L0_attn_W_kqv).T),
        "gate_wt": np.ascontiguousarray(np.asarray(L0_ffn_gate_w).T),
        "w_gate": np.ascontiguousarray(L0_ffn_w_gate),
        "w_up": np.ascontiguousarray(L0_ffn_w_up),
        "w_down": np.ascontiguousarray(L0_ffn_w_down),
        "sw_gate": np.ascontiguousarray(L0_ffn_sw_gate),
        "sw_up": np.ascontiguousarray(L0_ffn_sw_up),
        "sw_down": np.ascontiguousarray(L0_ffn_sw_down),
        "ident": np.eye(P, dtype=f32),
        "tri": np.triu(np.ones((P, P), f32), 1),
        "ali": ali,
    }
    nc = bacc.Bacc("TRN2", target_bir_lowering=False, num_devices=1)
    args = [nc.dram_tensor(f"in_{k}", a.shape, mybir.dt.from_np(a.dtype), kind="ExternalInput").ap()
            for k, a in arrays.items()]
    out = nc.dram_tensor("out_0", (T, D), F32, kind="ExternalOutput").ap()
    build(nc, *args, out)
    r = run_bass_kernel_spmd(nc, [{f"in_{k}": a for k, a in arrays.items()}], core_ids=[0])
    return r.results[0]["out_0"].reshape(B, S, D)
```

```python
from contextlib import ExitStack

import numpy as np
import concourse.bass as bass
from concourse import mybir

F32 = mybir.dt.float32
F32R = mybir.dt.float32r
I32 = mybir.dt.int32
ALU = mybir.AluOpType
ACT = mybir.ActivationFunctionType
AX = mybir.AxisListType
ds = bass.ds

P = 128
B, S, D = 8, 1024, 256
T = B * S
H, HD = 16, 16
E, F = 8, 352
NS = 2
KD = D // P
FC = [128, 128, 96]
NBLK = T // P
TT = 512
TB = TT // P
NT = T // TT
MOE_TILES = 2 * T // P + E
EPS = 1e-5
ROUTE_SCALE = 2.5
GU = 2 * F
DN = len(FC) * D
GROUPS = B * H // 4
GH = 4
HQ = S // 2
NK = S // P
QR = 4 * HD
S1_ROWS = QR + 2
S2_ROWS = QR + 3


def hold(eng, sem, value, passed):
    eng.wait_ge(sem, value).then_inc(passed, 1)


class Chain:

    def __init__(self, eng, sem, base=0, passed=None):
        self.eng, self.sem, self.base, self.passed, self.k = eng, sem, base, passed, 0

    def link(self, ins):
        ins.then_inc(self.sem, 1)
        self.k += 1
        if self.passed is None:
            self.eng.wait_ge(self.sem, self.base + self.k)
        else:
            hold(self.eng, self.sem, self.base + self.k, self.passed)


def steps(eng, n, unroll, emit, apart=1, lead=1):
    turns = (n - lead - apart) // unroll
    for j in range(lead):
        emit(j, j % unroll, j // unroll, j == 0, False)
    with eng.Fori(0, turns) as i:
        for u in range(lead, lead + unroll):
            emit(i * unroll + u, u % unroll, i + u // unroll, False, False)
    for j in range(lead + turns * unroll, n):
        emit(j, j % unroll, j // unroll, False, j == n - 1)


def build(nc, x, wqkv, gate_wt, w_gate, w_up, w_down, sw_gate, sw_up, sw_down, ident_in, tri_in, ali, out):
    with ExitStack() as kernel_ctx:
        def dram(name, shape, dt=F32):
            return nc.dram_tensor(name, shape, dt, kind="Internal").ap()

        scratch = dict(
            xn=dram("xn_scratch", [T, D]),
            qk=dram("qk_scratch", [2, 2 * D, T]),
            v=dram("v_scratch", [T, D]),
            lists=dram("lists_scratch", [E * T, 1], I32),
            ali=dram("ali_scratch", [H + 1, 2, S]),
            credit=dram("credit_scratch", [2, P, 1]),
            base=dram("base_scratch", [T, D]),
            yr=dram("yr_scratch", [MOE_TILES * P, D]),
        )

        def sb(name, shape, dt=F32):
            return kernel_ctx.enter_context(nc.sbuf_tensor(name, shape, dt))

        keep = dict(
            ctx=kernel_ctx,
            ident=sb("ident", [P, P]),
            logits=sb("logits", [P, NBLK * E]),
            pick=sb("pick", [P, 2, NBLK]),
            slot=sb("slot", [P, 2, NBLK]),
            count=sb("count", [P, E]),
            em8=sb("em8", [P, E]),
        )
        with ExitStack() as early_ctx:
            def sb(name, shape, dt=F32):
                return early_ctx.enter_context(nc.sbuf_tensor(name, shape, dt))

            keep.update(
                staging=(sb("gu32", [P, KD, GU]), sb("dn32", [P, DN])),
                shared_gu=[sb(f"shared_gu_{h}", [P, KD * NS * GU], F32R) for h in ("hi", "lo")],
                shared_dn=[sb(f"shared_dn_{h}", [P, NS * DN], F32R) for h in ("hi", "lo")],
                slot_i=sb("slot_i", [P, 2, NBLK], I32),
                token=sb("token", [P, NBLK], I32),
            )
            project(nc, keep, scratch, x, wqkv, gate_wt, sw_gate, sw_up, sw_down, ident_in, tri_in, ali)
            experts(nc, keep, scratch, x, w_gate, w_up, w_down)
        attend(nc, keep, scratch, out)


def expert_parts(staging, gu, dn, n_all, e):
    gu32, dn32 = staging
    wg = [w[:].rearrange("p (k e f) -> p k e f", k=KD, e=n_all)[:, :, e] for w in gu]
    return [(gu32[:], *wg)] + [(dn32[0:r, c0:c1], *(w[0:r, e * DN + c0:e * DN + c1] for w in dn))
                               for r, c0, c1 in ((P, 0, 2 * D), (FC[2], 2 * D, 3 * D))]


def load_expert(eng, staging, g, u, d, landed):
    gu32, dn32 = staging
    eng.dma_start(gu32[:, :, 0:F], g.rearrange("(k p) f -> p k f", p=P)).then_inc(landed, 16)
    eng.dma_start(gu32[:, :, F:2 * F], u.rearrange("(k p) f -> p k f", p=P)).then_inc(landed, 16)
    eng.dma_start(dn32[:, 0:2 * D].rearrange("p (c d) -> p c d", c=2),
                  d[0:2 * P].rearrange("(c p) d -> p c d", p=P)).then_inc(landed, 16)
    eng.dma_start(dn32[0:FC[2], 2 * D:3 * D], d[2 * P:F]).then_inc(landed, 16)


def stage(nc, ctx, keep):
    def sb(name, shape, dt=F32):
        return ctx.enter_context(nc.sbuf_tensor(name, shape, dt))

    def ps(name, shape, dt=F32):
        return ctx.enter_context(nc.psum_tensor(name, shape, dt))

    def sem(name):
        return keep["ctx"].enter_context(nc.semaphore(name))

    return sb, ps, sem


def project(nc, keep, scratch, x, wqkv, gate_wt, sw_gate, sw_up, sw_down, ident_in, tri_in, ali):
    with ExitStack() as ctx:
        sb, ps, sem = stage(nc, ctx, keep)
        ident, logits, pick, slot, count, em8 = (keep[k] for k in ("ident", "logits", "pick", "slot", "count", "em8"))
        w32, w_hi, w_lo = (sb(n, [P, KD, 3 * D + E], t) for n, t in (("w32", F32), ("w_hi", F32R), ("w_lo", F32R)))
        tri, ones = sb("tri", [P, P]), sb("ones", [P, P])
        x_sb = [sb(f"x{i}", [P, TB, D]) for i in range(2)]
        xn = [sb(f"xn{i}", [P, TB, D]) for i in range(2)]
        xt_hi = [sb(f"xt_hi{i}", [P, KD, TT], F32R) for i in range(2)]
        xt_lo = [sb(f"xt_lo{i}", [P, KD, TT], F32R) for i in range(2)]
        qk_out = [sb(f"qk_out{i}", [P, 2, 4, TT], F32R) for i in range(2)]
        v_out = [sb(f"v_out{i}", [P, TB, D]) for i in range(2)]
        stats, mv = sb("stats", [P, TB, 6]), sb("mv", [P, TB, 2])
        ve, root, newt, half = sb("ve", [P, TB]), sb("root", [P, TB]), sb("newt", [P, TB]), sb("half", [P, TB])
        lt, cmp_a, cmp_b, pos = (sb(n, [P, NBLK, E]) for n in ("lt", "cmp_a", "cmp_b", "pos"))
        top, chosen = sb("top", [P, NBLK]), sb("chosen", [P, 2, NBLK, E])
        both, carry, run = (sb(n, [P, E, NBLK]) for n in ("both", "carry", "run"))
        region = sb("region", [P, E])
        staging = [keep["staging"], (sb("gu32b", [P, KD, GU]), sb("dn32b", [P, DN]))]
        parts = [expert_parts(staging[i], keep["shared_gu"], keep["shared_dn"], NS, i) for i in range(NS)]
        zeros = cmp_a[:].rearrange("p n e -> p (n e)").bitcast(I32)

        p_xt = ps("p_xt", [P, KD, TT])
        p_qk = [ps(f"p_qk{i}", [P, TT]) for i in range(2)]
        p_v = ps("p_v", [P, TB, 512])

        names = ("w_in ali_st const_in iota_done x_in0 x_in1 ve_ready pow_ready xn_ready xt_ps xt_hi_ok xt_lo_ok "
                 "qk_ps qk_hi_ok qk_lo_ok v_ps v_ok g_read m_ready cnt_ps "
                 "passed xn_st0 xn_st1 qk_st0 qk_st1 v_st0 v_st1 zero_st dve_ln dve_sel dve_pro pool_pro "
                 "sw_in split_hi split")
        s = {n: sem("a_" + n) for n in names.split()}

        block = ctx.enter_context(nc.Block())

        @block.sync
        def _(sp):
            sp.dma_start(w32[:, :, 0:3 * D], wqkv.rearrange("(k p) n -> p k n", p=P)).then_inc(s["w_in"], 16)
            sp.dma_start(w32[:, :, 3 * D:], gate_wt.rearrange("(k p) e -> p k e", p=P)).then_inc(s["w_in"], 16)
            sp.dma_start(ident[:], ident_in).then_inc(s["const_in"], 16)
            sp.dma_start(tri[:], tri_in).then_inc(s["const_in"], 16)
            sp.dma_start(scratch["ali"], ali).then_inc(s["ali_st"], 16)
            for i in range(2):
                sp.sem_inc(s[f"qk_st{i}"], 16)
                sp.sem_inc(s[f"v_st{i}"], 16)
            vr = scratch["v"].rearrange("(n b p) d -> n p b d", p=P, b=TB)

            def tile(n, u, turn, first, last):
                pick_n = (lambda a, m: a[m]) if isinstance(n, int) else (
                    lambda a, m: a[ds(m, 1)].rearrange("o p b d -> p (o b) d"))
                if first:
                    for i in range(NS):
                        cols = slice(i * F, (i + 1) * F)
                        load_expert(sp, staging[i], sw_gate[:, cols], sw_up[:, cols], sw_down[cols], s["sw_in"])
                sp.wait_ge(s["qk_lo_ok"], 4 * n + 4)
                for hl in range(2):
                    sp.dma_start(scratch["qk"][hl].rearrange("(c p) t -> p c t", p=P)[:, :, ds(n * TT, TT)],
                                 qk_out[u][:, hl].bitcast(F32)).then_inc(s[f"qk_st{u}"], 16)
                sp.wait_ge(s["v_ok"], n + 1)
                sp.dma_start(pick_n(vr, n), v_out[u][:]).then_inc(s[f"v_st{u}"], 16)

            steps(sp, NT, 2, tile, apart=2)
            for i in range(2):
                sp.wait_ge(s[f"xn_st{i}"], 16 * (NT // 2))
                sp.wait_ge(s[f"qk_st{i}"], 32 * (NT // 2) + 16)
                sp.wait_ge(s[f"v_st{i}"], 16 * (NT // 2 + 1))
            sp.wait_ge(s["ali_st"], 16)
            sp.wait_ge(s["zero_st"], 16)

        @block.gpsimd
        def _(pool):
            g = nc.gpsimd
            xr = x.rearrange("(n b p) d -> n p b d", p=P, b=TB)
            xnr = scratch["xn"].rearrange("(n b p) d -> n p b d", p=P, b=TB)
            at = lambda a, m: a[m] if isinstance(m, int) else a[ds(m, 1)].rearrange("o p b d -> p (o b) d")

            def load(n, u):
                pool.dma_start(x_sb[u][:], at(xr, n)).then_inc(s[f"x_in{u}"], 16)

            def store(n, u):
                hold(pool, s["xn_ready"], n + 1, s["passed"])
                pool.dma_start(at(xnr, n), xn[u][:]).then_inc(s[f"xn_st{u}"], 16)

            load(0, 0)
            load(1, 1)
            g.memset(ones[:], 1.0).then_inc(s["iota_done"], 1)
            g.memset(half[:], -0.5).then_inc(s["iota_done"], 1)
            g.iota(em8[:], [[1, E]], base=-E, channel_multiplier=0,
                   allow_small_or_imprecise_dtypes=True).then_inc(s["iota_done"], 1)
            g.iota(region[:], [[T, E]], base=0, channel_multiplier=0,
                   allow_small_or_imprecise_dtypes=True).then_inc(s["iota_done"], 1)
            g.iota(keep["token"][:], [[P, NBLK]], base=0, channel_multiplier=1).then_inc(s["iota_done"], 1)
            g.memset(zeros, 0).then_inc(s["pool_pro"], 1)
            pool.wait_ge(s["pool_pro"], 1)
            g.dma_start(scratch["lists"].rearrange("(p n) o -> p (n o)", p=P), zeros).then_inc(s["zero_st"], 16)
            pool.wait_ge(s["iota_done"], 5)

            def power(n):
                hold(pool, s["ve_ready"], n + 1, s["passed"])
                g.tensor_tensor(root[:], ve[:], half[:], ALU.pow).then_inc(s["pow_ready"], 1)

            for n in range(2):
                power(n)
                store(n, n)
                load(n + 2, n)

            def tile(n, u, turn, first, last):
                if not (isinstance(n, int) and n + 2 >= NT):
                    power(n + 2)
                    store(n + 2, u)
                    if not (isinstance(n, int) and n + 4 >= NT):
                        load(n + 4, u)

            steps(pool, NT, 2, tile, apart=4)
            pool.wait_ge(s["split_hi"], 3 * NS)
            for i in range(NS):
                for src, hi, lo in parts[i]:
                    g.tensor_tensor(lo, src, hi.bitcast(F32), ALU.subtract).then_inc(s["split"], 1)
            pool.wait_ge(s["split"], 3 * NS)

        @block.vector
        def _(dve):
            v = nc.vector
            pro = Chain(dve, s["dve_pro"])

            LN_LINKS = 6

            def moments(n, u, turn):
                c = Chain(dve, s["dve_ln"], n * LN_LINKS, s["passed"])
                dve.wait_ge(s[f"x_in{u}"], 16 * (turn + 1))
                for b in range(TB):
                    last = v.bn_stats(stats[:, b], x_sb[u][:, b])
                c.link(last)
                for b in range(TB):
                    last = v.bn_aggr(mv[:, b], stats[:, b])
                c.link(last)
                v.tensor_scalar(ve[:], mv[:, :, 1], EPS, None, ALU.add).then_inc(s["ve_ready"], 1)
                return c

            def normalise(c, n, u, turn):
                dve.wait_ge(s["pow_ready"], n + 1)
                c.link(v.tensor_tensor(newt[:], root[:], root[:], ALU.mult))
                c.link(v.tensor_tensor(newt[:], newt[:], ve[:], ALU.mult))
                c.link(v.tensor_scalar(newt[:], newt[:], -0.5, 1.5, ALU.mult, ALU.add))
                c.link(v.tensor_tensor(newt[:], newt[:], root[:], ALU.mult))
                if not (isinstance(n, int) and n < 2):
                    dve.wait_ge(s[f"xn_st{u}"], 16 * turn)
                for b in range(TB):
                    last = v.tensor_scalar(xn[u][:, b], x_sb[u][:, b], mv[:, b, 0:1], newt[:, b:b + 1],
                                           ALU.subtract, ALU.mult)
                last.then_inc(s["xn_ready"], 1)
                assert c.k == LN_LINKS

            normalise(moments(0, 0, 0), 0, 0, 0)
            dve.wait_ge(s["w_in"], 32)
            pro.link(v.tensor_copy(w_hi[:], w32[:]))
            pro.link(v.tensor_tensor(w_lo[:], w32[:], w_hi[:].bitcast(F32), ALU.subtract))

            def split_x(n, u):
                dve.wait_ge(s["xt_hi_ok"], n + 1)
                v.tensor_tensor(xt_lo[u][:], p_xt[:], xt_hi[u][:].bitcast(F32), ALU.subtract).then_inc(s["xt_lo_ok"], 1)

            split_x(0, 0)
            normalise(moments(1, 1, 0), 1, 1, 0)

            def tile(n, u, turn, first, last):
                ahead = not (isinstance(n, int) and n + 2 >= NT)
                if ahead:
                    c = moments(n + 2, u, turn + 1)
                for chunk in range(4):
                    if chunk == 2:
                        if not last:
                            split_x(n + 1, 1 - u)
                        if ahead:
                            normalise(c, n + 2, u, turn + 1)
                    dve.wait_ge(s["qk_hi_ok"], 4 * n + (chunk + 1))
                    v.scalar_tensor_tensor(qk_out[u][:, 1, chunk], p_qk[chunk % 2][:], 1.0 if chunk < 2 else 1 / 16,
                                           qk_out[u][:, 0, chunk].bitcast(F32), ALU.mult,
                                           ALU.subtract).then_inc(s["qk_lo_ok"], 1)

            steps(dve, NT, 2, tile, apart=2)
            c = Chain(dve, s["dve_sel"])
            dve.wait_ge(s["iota_done"], 5)
            c.link(v.memset(carry[:], 1.0))
            c.link(v.memset(carry[:, :, 0:1], 0.0))
            dve.wait_ge(s["g_read"], NT)
            dve.wait_ge(s["zero_st"], 16)
            lg = logits[:].rearrange("p (n e) -> p n e", e=E)
            em = em8[:, None, :].to_broadcast([P, NBLK, E])
            wide = lambda a: a[:, :, None].to_broadcast([P, NBLK, E])

            def pick_top(src, k):
                c.link(v.tensor_reduce(top[:], src, AX.X, ALU.max))
                c.link(v.tensor_tensor(cmp_a[:], src, wide(top), ALU.is_equal))
                c.link(v.tensor_tensor(cmp_b[:], cmp_a[:], em, ALU.mult))
                c.link(v.tensor_reduce(pick[:, k], cmp_b[:], AX.X, ALU.min))
                c.link(v.tensor_tensor(chosen[:, k], em, wide(pick[:, k]), ALU.is_equal))

            pick_top(lg, 0)
            c.link(v.scalar_tensor_tensor(lt[:], chosen[:, 0], -1e30, lg, ALU.mult, ALU.add))
            pick_top(lt[:], 1)
            v.tensor_tensor(both[:].rearrange("p e n -> p n e"), chosen[:, 0], chosen[:, 1],
                            ALU.add).then_inc(s["m_ready"], 1)
            dve.wait_ge(s["cnt_ps"], 1)
            before = p_qk[0][:].rearrange("p (e n) -> p n e", e=E)
            total = p_qk[1][:]
            flat = run[:].rearrange("p e n -> p (e n)")
            c.link(v.tensor_tensor_scan(flat, carry[:].rearrange("p e n -> p (e n)"), total, 0.0, ALU.mult, ALU.add))
            v.tensor_copy(count[:], run[:, :, NBLK - 1])
            c.link(v.tensor_tensor(both[:].rearrange("p e n -> p (e n)"), flat, total, ALU.subtract))
            c.link(v.tensor_tensor(pos[:], before, both[:].rearrange("p e n -> p n e"), ALU.add))
            c.link(v.tensor_tensor(pos[:], pos[:], region[:, None, :].to_broadcast([P, NBLK, E]), ALU.add))
            for k in range(2):
                c.link(v.tensor_tensor(cmp_b[:], pos[:], chosen[:, k], ALU.mult))
                c.link(v.tensor_reduce(slot[:, k], cmp_b[:], AX.X, ALU.add))
            v.tensor_copy(keep["slot_i"][:], slot[:])

        @block.scalar
        def _(act):
            a = nc.scalar

            def split_x(n, u):
                act.wait_ge(s["xt_ps"], n + 1)
                a.copy(xt_hi[u][:], p_xt[:]).then_inc(s["xt_hi_ok"], 1)

            split_x(0, 0)

            def tile(n, u, turn, first, last):
                act.wait_ge(s[f"qk_st{u}"], 32 * turn + 16)
                for c in range(4):
                    if c == 2 and not last:
                        split_x(n + 1, 1 - u)
                    act.wait_ge(s["qk_ps"], 4 * n + (c + 1))
                    a.mul(qk_out[u][:, 0, c], p_qk[c % 2][:], 1.0 if c < 2 else 1 / 16).then_inc(s["qk_hi_ok"], 1)
                act.wait_ge(s[f"v_st{u}"], 16 * (turn + 1))
                act.wait_ge(s["v_ps"], n + 1)
                a.copy(v_out[u][:], p_v[:, :, 0:D]).then_inc(s["v_ok"], 1)
                a.copy(logits[:, ds(n * TB * E, TB * E)].rearrange("p (b e) -> p b e", b=TB),
                       p_v[:, :, D:D + E]).then_inc(s["g_read"], 1)
                if isinstance(n, int) and n >= NT - NS - 1 and not last:
                    act.wait_ge(s["sw_in"], 64 * NS)
                    for src, hi, lo in parts[n - (NT - NS - 1)]:
                        a.copy(hi, src).then_inc(s["split_hi"], 1)

            steps(act, NT, 2, tile, apart=NS + 1)

        @block.tensor
        def _(pe):
            t = nc.tensor
            pe.wait_ge(s["const_in"], 32)

            def turn_x(n, u):
                pe.wait_ge(s["xn_ready"], n + 1)
                for b in range(TB):
                    for k in range(KD):
                        last = t.transpose(p_xt[:, k, b * P:(b + 1) * P], xn[u][:, b, k * P:(k + 1) * P], ident[:])
                last.then_inc(s["xt_ps"], 1)

            turn_x(0, 0)
            pe.wait_ge(s["dve_pro"], 2)

            def products(dst, lhs, rhs):
                n = 0
                for k in range(KD):
                    for a, b in ((0, 0), (0, 1), (1, 0)):
                        last = t.matmul(dst, lhs[a](k), rhs[b](k), start=(n == 0), stop=(n == 3 * KD - 1))
                        n += 1
                return last

            def tile(n, u, turn, first, last):
                pe.wait_ge(s["xt_lo_ok"], n + 1)
                xs = lambda b: [lambda k, w=w: w[u][:, k, b * P:(b + 1) * P] for w in (xt_hi, xt_lo)]
                for c in range(4):
                    if c == 2 and not last:
                        turn_x(n + 1, 1 - u)
                    if not (first and c < 2):
                        pe.wait_ge(s["qk_lo_ok"], 4 * n + c - 1)
                    products(p_qk[c % 2][:], [lambda k, w=w: w[:, k, c * P:(c + 1) * P] for w in (w_hi, w_lo)],
                             [lambda k, w=w: w[u][:, k] for w in (xt_hi, xt_lo)]).then_inc(s["qk_ps"], 1)
                if not first:
                    pe.wait_ge(s["v_ok"], n)
                    pe.wait_ge(s["g_read"], n)
                for b in range(TB):
                    ins = products(p_v[:, b, 0:D + E], xs(b), [lambda k, w=w: w[:, k, 2 * D:] for w in (w_hi, w_lo)])
                ins.then_inc(s["v_ps"], 1)

            steps(pe, NT, 2, tile)
            pe.wait_ge(s["m_ready"], 1)
            pe.wait_ge(s["iota_done"], 5)
            chosen_by = both[:].rearrange("p e n -> p (e n)")
            t.matmul(p_qk[0][:], tri[:], chosen_by, start=True, stop=True)
            t.matmul(p_qk[1][:], ones[:], chosen_by, start=True, stop=True).then_inc(s["cnt_ps"], 1)


def experts(nc, keep, scratch, x, w_gate, w_up, w_down):
    with ExitStack() as ctx:
        sb, ps, sem = stage(nc, ctx, keep)
        ident, count, em8 = keep["ident"], keep["count"], keep["em8"]
        wgu = [sb(f"wgu_{h}", [P, KD * E * GU], F32R) for h in ("hi", "lo")]
        wdn = [sb(f"wdn_{h}", [P, E * DN], F32R) for h in ("hi", "lo")]
        slot_c, token_c = sb("slot_c", [P, 2, TB], I32), sb("token_c", [P, TB], I32)
        XB = 4
        x_sb = [sb(f"xe{i}", [P, D]) for i in range(XB)]
        ids = [sb(f"ids{i}", [P, 1], I32) for i in range(XB)]
        xt = [[sb(f"xet_{h}{i}", [P, KD, P], F32R) for i in range(2)] for h in ("hi", "lo")]
        gated, h_sb = sb("gated", [P, F]), sb("h_sb", [P, F])
        ht = [[sb(f"ht_{h}{i}", [P, 3, P], F32R) for i in range(2)] for h in ("hi", "lo")]
        y_sb = [sb(f"y{i}", [P, D]) for i in range(XB)]
        tile_no = sb("tile_no", [1, MOE_TILES])
        stg = keep["staging"][1]
        t_exp, t_cmp, t_blk = (stg[0:1, i * MOE_TILES:(i + 1) * MOE_TILES] for i in range(3))
        w_off_i, blk_i = sb("w_off_i", [1, 2, MOE_TILES], I32), sb("blk_i", [1, MOE_TILES], I32)
        nt_i, nt_f = sb("nt_i", [P, E], I32), sb("nt_f", [P, E])
        base, end, one8 = sb("base", [P, E]), sb("end", [P, E]), sb("one8", [P, E])
        adj, back = sb("adj", [P, E]), sb("back", [P, E])
        yslot = stg[:, 3 * MOE_TILES:3 * MOE_TILES + 2 * NBLK].rearrange("p (k n) -> p k n", k=2)
        keep_slot, pick = keep["slot"], keep["pick"]

        p_x = ps("pe_x", [P, KD, P])
        p_gate, p_up = ps("p_gate", [P, 512]), ps("p_up", [P, 512])
        p_h, p_y = ps("pe_h", [P, 3, P]), ps("pe_y", [P, 512])

        names = ("passed w_in split tab tiles_ready pool_pro copied scat")
        s = {n: sem("e_" + n) for n in names.split()}

        block = ctx.enter_context(nc.Block())

        def stream(name, more):
            ns = (more + " x_in0 x_in1 x_in2 x_in3 xt_ps xt_hi xt_lo gate_ps up_ps gated h_ok "
                  "ht_ps ht_hi ht_lo y_ps y_free y_st0 y_st1 y_st2 y_st3")
            return {n: sem(f"{name}_{n}") for n in ns.split()}

        sh, rt = stream("sh", "r_in0 r_in1 r_in2 r_in3"), stream("rt", "id_in0 id_in1 id_in2 id_in3")

        def io(eng, q, n, src, dst, ids_of=None, residual=None):
            def load(j, u, free):
                if free is not None:
                    eng.wait_ge(q["xt_ps"], free)
                if ids_of is None:
                    eng.dma_start(x_sb[u][:], src[ds(j * P, P)]).then_inc(q[f"x_in{u}"], 16)
                else:
                    blk = eng.value_load(ids_of[0:1, ds(j, 1)], min_val=0, max_val=E * T // P - 1)
                    eng.dma_start(ids[u][:], src[ds(blk * P, P)]).then_inc(q[f"id_in{u}"], 16)

            for i in range(XB):
                eng.sem_inc(q[f"y_st{i}"], 16)
            for j in range(XB - 1):
                load(j, j, None)

            def load_residual(j, u, turn):
                eng.wait_ge(q[f"y_st{u}"], 16 * (turn + 1))
                eng.dma_start(y_sb[u][:], residual[ds(j * P, P)]).then_inc(q[f"r_in{u}"], 16)

            if residual is not None:
                load_residual(0, 0, 0)
                load_residual(1, 1, 0)

            def step(j, u, turn, first, last):
                if isinstance(j, int) and j > 4:
                    if j + XB - 1 < n:
                        load(j + XB - 1, (u + XB - 1) % XB, j)
                else:
                    load(j + XB - 1, (u + XB - 1) % XB, None if first else j)
                if not first:
                    store(j - 1, (u - 1) % XB)
                if residual is not None and not (isinstance(j, int) and j + 2 >= n):
                    load_residual(j + 2, (u + 2) % XB, turn + (u + 2) // XB)

            def store(j, u):
                eng.wait_ge(q["y_free"], j + 2)
                eng.dma_start(dst[ds(j * P, P)], y_sb[u][:]).then_inc(q[f"y_st{u}"], 16)

            steps(eng, n, XB, step, apart=XB - 1)
            store(n - 1, (n - 1) % XB)
            for i in range(XB):
                eng.wait_ge(q[f"y_st{i}"], 16 * (n // XB + 1))

        TILE_LINKS = 9

        def tables(c):
            g = nc.gpsimd
            c.link(g.tensor_scalar(t_exp, tile_no[:], end[0:1, 0:1], None, ALU.is_ge))
            for e in range(1, E - 1):
                c.link(g.tensor_scalar(t_cmp, tile_no[:], end[0:1, e:e + 1], None, ALU.is_ge))
                c.link(g.tensor_tensor(t_exp, t_exp, t_cmp, ALU.add))
            c.link(g.tensor_copy(t_blk, tile_no[:]))
            for e in range(E):
                c.link(g.tensor_scalar(t_cmp, t_exp, float(e), adj[0:1, e:e + 1], ALU.is_equal, ALU.mult))
                c.link(g.tensor_tensor(t_blk, t_blk, t_cmp, ALU.add))
            c.link(g.tensor_scalar(blk_i[:], t_blk, float(E * T // P - 1), None, ALU.min))
            c.link(g.tensor_scalar(w_off_i[:, 0], t_exp, float(GU), None, ALU.mult))
            c.link(g.tensor_scalar(w_off_i[:, 1], t_exp, float(DN), None, ALU.mult))
            c.link(g.tensor_copy(yslot, keep_slot[:]))
            for e in range(E):
                for k in range(2):
                    c.link(g.tensor_scalar(keep_slot[:, k], pick[:, k], float(e - E), back[:, e:e + 1],
                                           ALU.is_equal, ALU.mult))
                    c.link(g.tensor_tensor(yslot[:, k], yslot[:, k], keep_slot[:, k], ALU.add))
            g.tensor_copy(keep_slot[:], yslot).then_inc(s["tiles_ready"], 1)

        @block.gpsimd
        def _(pool):
            g = nc.gpsimd
            g.memset(one8[:], 1.0).then_inc(s["pool_pro"], 1)
            g.iota(tile_no[:], [[1, MOE_TILES]], base=0, channel_multiplier=0,
                   allow_small_or_imprecise_dtypes=True).then_inc(s["pool_pro"], 1)
            with pool.Fori(0, NT) as n:
                g.tensor_copy(slot_c[:], keep["slot_i"][:, :, ds(n * TB, TB)]).then_inc(s["copied"], 1)
                g.tensor_copy(token_c[:], keep["token"][:, ds(n * TB, TB)]).then_inc(s["copied"], 1)
                hold(pool, s["copied"], 2 * n + 2, s["passed"])
                for c in range(2):
                    for b in range(TB):
                        g.indirect_dma_start(
                            scratch["lists"], bass.IndirectOffsetOnAxis(slot_c[:, c, b:b + 1], 0),
                            token_c[:, b:b + 1], None).then_inc(s["scat"], 16)
                hold(pool, s["scat"], n * (16 * 2 * TB) + 16 * 2 * TB, s["passed"])
            for e in range(E):
                load_expert(pool, keep["staging"], w_gate[e], w_up[e], w_down[e], s["w_in"])
                pool.wait_ge(s["w_in"], 64 * (e + 1))
                parts = expert_parts(keep["staging"], wgu, wdn, E, e)
                for src, hi, lo in parts:
                    g.tensor_copy(hi, src).then_inc(s["split"], 1)
                pool.wait_ge(s["split"], 6 * e + 3)
                for src, hi, lo in parts:
                    g.tensor_tensor(lo, src, hi.bitcast(F32), ALU.subtract).then_inc(s["split"], 1)
                pool.wait_ge(s["split"], 6 * e + 6)
            pool.wait_ge(s["tab"], TILE_LINKS)
            tables(Chain(pool, s["tab"], TILE_LINKS))
            def step(j, u, turn, first, last):
                hold(pool, rt[f"id_in{u}"], 16 * (turn + 1), s["passed"])
                g.indirect_dma_start(x_sb[u][:], None, scratch["xn"],
                                     bass.IndirectOffsetOnAxis(ids[u][:], 0)).then_inc(rt[f"x_in{u}"], 16)
            steps(pool, MOE_TILES, XB, step)

        def pe_stream(pe, q, n, subs, gu, dn, gu_off, dn_off):
            t = nc.tensor
            n_exp = NS if subs == NS else E

            def turn_x(j, u, turn):
                pe.wait_ge(q[f"x_in{u}"], 16 * (turn + 1))
                for k in range(KD):
                    last = t.transpose(p_x[:, k], x_sb[u][:, k * P:(k + 1) * P], ident[:])
                last.then_inc(q["xt_ps"], 1)

            def project_up(j, u, off, up):
                i = 0
                for k in range(KD):
                    for a, b in ((0, 0), (0, 1), (1, 0)):
                        ins = t.matmul((p_gate, p_up)[up][:, 0:F], xt[a][u % 2][:, k],
                                       gu[b][:, ds(off + (k * n_exp * GU + up * F), F)],
                                       start=(i == 0), stop=(i == 3 * KD - 1))
                        i += 1
                ins.then_inc(q["up_ps" if up else "gate_ps"], 1)

            def turn_h(job):
                pe.wait_ge(q["h_ok"], job + 1)
                for c, rows in enumerate(FC):
                    ins = t.transpose(p_h[0:rows, c], h_sb[:, c * P:c * P + rows], ident[:])
                ins.then_inc(q["ht_ps"], 1)

            def down(j, sub, par, off):
                pe.wait_ge(q["ht_lo"], subs * j + sub + 1)
                if sub == 0:
                    pe.wait_ge(q["y_free"], j + 1)
                i, all_ = 0, 3 * len(FC)
                for c, rows in enumerate(FC):
                    for a, b in ((0, 0), (0, 1), (1, 0)):
                        last = t.matmul(p_y[:, 0:D], ht[a][par][0:rows, c], dn[b][0:rows, ds(off + c * D, D)],
                                        start=(i == 0 and sub == 0), stop=(i == all_ - 1 and sub == subs - 1))
                        i += 1
                if sub == subs - 1:
                    last.then_inc(q["y_ps"], 1)

            def step(j, u, turn, first, last):
                if first:
                    turn_x(0, 0, 0)
                for sub in range(subs):
                    job = subs * j + sub
                    if not (isinstance(job, int) and job < 2):
                        jd = j - (2 // subs)
                        down(jd, sub, job_parity(subs, u % 2, sub), dn_off(pe, jd, sub))
                    off = gu_off(pe, j, sub)
                    if not (first and sub == 0):
                        turn_h(job - 1)
                    if sub == 0:
                        pe.wait_ge(q["xt_lo"], j + 1)
                    project_up(j, u, off, 0)
                    if sub == 0 and not last:
                        turn_x(j + 1, (u + 1) % XB, turn + (1 if u == XB - 1 else 0))
                    project_up(j, u, off, 1)

            steps(pe, n, XB, step, lead=2)
            jobs = subs * n
            for job in (jobs - 2, jobs - 1):
                if job == jobs - 1:
                    turn_h(job)
                j, sub = divmod(job, subs)
                down(j, sub, job % 2, dn_off(pe, j, sub))

        def job_parity(subs, par, sub):
            return par if subs == 1 else sub

        def act_stream(act, q, n, subs):
            a = nc.scalar

            def split_x(j, par):
                act.wait_ge(q["xt_ps"], j + 1)
                a.copy(xt[0][par][:], p_x[:]).then_inc(q["xt_hi"], 1)

            def step(j, u, turn, first, last):
                par = u % 2
                if first:
                    split_x(0, 0)
                for sub in range(subs):
                    job = subs * j + sub
                    act.wait_ge(q["gate_ps"], job + 1)
                    a.activation(gated[:], p_gate[:, 0:F], ACT.Silu).then_inc(q["gated"], 1)
                    if sub == 0 and not last:
                        split_x(j + 1, 1 - par)
                    act.wait_ge(q["ht_ps"], job + 1)
                    jp = job_parity(subs, par, sub)
                    a.copy(ht[0][jp][:, 0:2], p_h[:, 0:2])
                    a.copy(ht[0][jp][0:FC[2], 2], p_h[0:FC[2], 2]).then_inc(q["ht_hi"], 1)

            steps(act, n, XB, step)

        def dve_stream(dve, q, n, subs):
            v = nc.vector

            def split_x(j, par):
                dve.wait_ge(q["xt_hi"], j + 1)
                v.tensor_tensor(xt[1][par][:], p_x[:], xt[0][par][:].bitcast(F32), ALU.subtract).then_inc(q["xt_lo"], 1)

            def finish(j, u, turn):
                dve.wait_ge(q["y_ps"], j + 1)
                if subs == NS:
                    dve.wait_ge(q[f"r_in{u}"], 16 * (turn + 1))
                    v.tensor_tensor(y_sb[u][:], p_y[:, 0:D], y_sb[u][:], ALU.add).then_inc(q["y_free"], 1)
                else:
                    dve.wait_ge(q[f"y_st{u}"], 16 * (turn + 1))
                    v.tensor_copy(y_sb[u][:], p_y[:, 0:D]).then_inc(q["y_free"], 1)

            dve.sem_inc(q["y_free"], 1)

            def step(j, u, turn, first, last):
                par = u % 2
                if first:
                    split_x(0, 0)
                for sub in range(subs):
                    job = subs * j + sub
                    if sub == 0 and not last:
                        split_x(j + 1, 1 - par)
                    dve.wait_ge(q["gated"], job + 1)
                    dve.wait_ge(q["up_ps"], job + 1)
                    v.tensor_tensor(h_sb[:], p_up[:, 0:F], gated[:], ALU.mult).then_inc(q["h_ok"], 1)
                    if sub == 0 and not first:
                        finish(j - 1, (u - 1) % XB, turn - (1 if u == 0 else 0))
                    dve.wait_ge(q["ht_hi"], job + 1)
                    jp = job_parity(subs, par, sub)
                    v.tensor_tensor(ht[1][jp][:, 0:2], p_h[:, 0:2], ht[0][jp][:, 0:2].bitcast(F32), ALU.subtract)
                    v.tensor_tensor(ht[1][jp][0:FC[2], 2], p_h[0:FC[2], 2], ht[0][jp][0:FC[2], 2].bitcast(F32),
                                    ALU.subtract).then_inc(q["ht_lo"], 1)
                if last:
                    finish(j, u, turn)

            steps(dve, n, XB, step)

        @block.sync
        def _(sp):
            io(sp, sh, NBLK, scratch["xn"], scratch["base"], None, x)
            sp.wait_ge(s["tiles_ready"], 1)
            sp.wait_ge(s["scat"], 16 * 2 * NBLK)
            io(sp, rt, MOE_TILES, scratch["lists"], scratch["yr"], blk_i)

        @block.vector
        def _(dve):
            v = nc.vector
            c = Chain(dve, s["tab"])
            dve.wait_ge(s["pool_pro"], 2)
            c.link(v.tensor_scalar(nt_f[:], count[:], float(P - 1), None, ALU.add))
            c.link(v.tensor_copy(nt_i[:], nt_f[:]))
            c.link(v.tensor_scalar(nt_i[:], nt_i[:], 7, None, ALU.arith_shift_right))
            c.link(v.tensor_copy(nt_f[:], nt_i[:]))
            c.link(v.tensor_tensor_scan(end[:], one8[:], nt_f[:], 0.0, ALU.mult, ALU.add))
            c.link(v.tensor_tensor(base[:], end[:], nt_f[:], ALU.subtract))
            c.link(v.tensor_scalar(adj[:], em8[:], float(T // P), float(T // P * E), ALU.mult, ALU.add))
            c.link(v.tensor_tensor(adj[:], adj[:], base[:], ALU.subtract))
            c.link(v.tensor_scalar(back[:], adj[:], float(-P), None, ALU.mult))
            assert c.k == TILE_LINKS
            dve_stream(dve, sh, NBLK, NS)
            dve_stream(dve, rt, MOE_TILES, 1)

        @block.scalar
        def _(act):
            act_stream(act, sh, NBLK, NS)
            act_stream(act, rt, MOE_TILES, 1)

        @block.tensor
        def _(pe):
            pe_stream(pe, sh, NBLK, NS, keep["shared_gu"], keep["shared_dn"],
                      lambda pe, j, sub: sub * GU, lambda pe, j, sub: sub * DN)
            pe.wait_ge(s["split"], 6 * E)
            pe.wait_ge(s["tiles_ready"], 1)

            def offset(row, most):
                return lambda pe, j, sub: pe.value_load(w_off_i[0:1, row, ds(j, 1)], min_val=0, max_val=most)

            pe_stream(pe, rt, MOE_TILES, 1, wgu, wdn, offset(0, (E - 1) * GU), offset(1, (E - 1) * DN))


def attend(nc, keep, scratch, out):
    with ExitStack() as ctx:
        sb, ps, sem = stage(nc, ctx, keep)
        ident, logits, pick, slot, em8 = (keep[k] for k in ("ident", "logits", "pick", "slot", "em8"))
        NB_OP = 3
        k_op = [sb(f"k_op{i}", [S2_ROWS, GH, S], F32R) for i in range(NB_OP)]
        q_op = [sb(f"q_op{i}", [96, GH, S], F32R) for i in range(NB_OP)]
        v_in = [sb(f"v_in{i}", [P, NK, GH * HD]) for i in range(NB_OP)]
        v_op = [sb(f"v_op{i}", [P, NK, GH, 32]) for i in range(NB_OP)]
        probs = [sb(f"probs{i}", [P, GH, HQ]) for i in range(4)]
        neg = [sb(f"neg{i}", [P, 4], F32R) for i in range(2)]
        m_row = [sb(f"m_row{i}", [4, P], F32R) for i in range(4)]
        o_sb = [sb(f"o_sb{i}", [P, HQ]) for i in range(2)]
        rec = sb("rec", [P, 4, GH])
        att = sb("att", [P, 2 * NK, D])
        base_c = [sb(f"base_c{i}", [P, D]) for i in range(2)]
        y_c = [[sb(f"y_c{k}{i}", [P, D]) for i in range(2)] for k in range(2)]
        fin = sb("fin", [P, 3, NK, D])
        slot_i = sb("yslot_i", [P, 2, NBLK], I32)
        col_i = [sb(f"col_i{i}", [P, 2], I32) for i in range(2)]
        col_w = [sb(f"col_w{i}", [P, 2]) for i in range(2)]
        wts = sb("wts", [P, 2, NBLK])
        ex, cmp_ = (fin[:, 0, 2 * i:2 * i + 2].rearrange("p q d -> p (q d)").rearrange("p (n e) -> p n e", e=E)
                    for i in range(2))
        t64, z64 = sb("t64", [P, NBLK]), sb("z64", [P, NBLK])

        p1 = [ps(f"p1_{i}", [P, S]) for i in range(2)]
        p2 = [ps(f"p2_{i}", [P, 512]) for i in range(3)]
        p_o = ps("p_o", [P, HQ])

        names = ("passed ones_in init init_v s1_ps s1_read s2_ps s2_read m_ok pv_done v_ok o_ok rec_ok att_ok sub_ok "
                 "ex_ok w_ready dve_w pool_c o_st0 o_st1 c_ok base_in0 base_in1 yg_in0 yg_in1 fin_base fin_y "
                 "dve_f fin_ok fin_st")
        s = {n: sem("t_" + n) for n in names.split()}
        k_in = [sem(f"t_k_in{u}") for u in range(NB_OP)]
        v_in_s = [sem(f"t_v_in{u}") for u in range(NB_OP)]
        m_in = [sem(f"t_m_in{c}") for c in range(4)]

        UNITS = 2 * NK * GH
        HALF = UNITS // 2
        MAX_UNITS = 2 * GH * 4
        CHUNK = 4
        CHUNKS = MAX_UNITS // CHUNK
        AHEAD = [MAX_UNITS * (n + 1) // UNITS for n in range(UNITS)]
        TURN_AT = {2 * CHUNK * c + 14: c for c in range(CHUNKS - 1)}
        OWN_TURN = 6
        OUT_COPY, OUT_TURN = 2, 14
        V_SPREAD = 20
        R1 = MAX_UNITS + 2
        R2 = UNITS + CHUNKS

        def ring1(g, first):
            return MAX_UNITS if first else g * R1 + (MAX_UNITS - 1)

        def bank1(first, r):
            return ((MAX_UNITS if first else MAX_UNITS - 1) + r) % 2

        def ring2(g):
            return g * R2 + (CHUNKS - 1)

        def bank2(r):
            return (CHUNKS - 1 + r) % 3

        assert R1 % 2 == 0 and R2 % 3 == 0

        def groups(eng, emit):
            turns = (GROUPS - 2) // 3
            assert turns * 3 == GROUPS - 2
            emit(0, 0, 0, False, True)
            with eng.Fori(0, turns) as i:
                for r in range(3):
                    emit(i * 3 + (1 + r), (1 + r) % 3, i + (1 + r) // 3, True, True)
            emit(GROUPS - 1, (GROUPS - 1) % 3, (GROUPS - 1) // 3, True, False)

        def following(u, turn):
            return (u + 1) % 3, turn + (1 if u == 2 else 0)

        block = ctx.enter_context(nc.Block())

        @block.sync
        def _(sp):
            qk, ali = scratch["qk"], scratch["ali"]
            for i in range(NB_OP):
                sp.dma_start(k_op[i][QR + 2:QR + 3].bitcast(F32),
                             ali[H:H + 1, 0:1].to_broadcast([1, GH, S])).then_inc(s["ones_in"], 16)

            def load(g, u):
                b, hg = g // (H // GH), g % (H // GH)
                for base, op, parts in ((0, k_op, (0, 1, 0, 1)), (D, q_op, (0, 0, 1, 1))):
                    for r, hl in enumerate(parts):
                        sp.dma_start(op[u][r * HD:(r + 1) * HD].bitcast(F32),
                                     qk[hl][ds(hg * (GH * HD) + base, GH * HD), ds(b * S, S)]
                                     .rearrange("(h d) t -> d h t", d=HD)).then_inc(k_in[u], 16)
                sp.dma_start(k_op[u][QR:QR + 2].bitcast(F32),
                             ali[ds(hg * GH, GH)].rearrange("h a t -> a h t")).then_inc(k_in[u], 16)
                sp.dma_start(v_in[u][:], scratch["v"][ds(b * S, S), ds(hg * (GH * HD), GH * HD)]
                             .rearrange("(k p) c -> p k c", p=P)).then_inc(v_in_s[u], 16)

            def send_max(g, u, chunks):
                for c in chunks:
                    half, h = divmod(c, GH)
                    sp.wait_ge(s["m_ok"], g * CHUNKS + (c + 1))
                    sp.dma_start(q_op[u][QR + 2:QR + 3, h, half * HQ:(half + 1) * HQ]
                                 .rearrange("o (q c) -> o q c", q=4).bitcast(F32),
                                 m_row[c % 4][:].bitcast(F32)).then_inc(m_in[c % 4], 16)

            load(0, 0)
            load(1, 1)
            sp.wait_ge(s["init"], NB_OP)
            send_max(0, 0, range(CHUNKS - 1))

            def group(g, u, turn, has_prev, has_next):
                if has_next and not (isinstance(g, int) and g + 2 >= GROUPS):
                    if has_prev:
                        sp.wait_ge(s["pv_done"], g * (2 * NK) + NK)
                    load((g + 2) % GROUPS, (u + 2) % 3)
                send_max(g, u, [CHUNKS - 1])
                if has_next:
                    send_max(g + 1, following(u, turn)[0], range(CHUNKS - 1))

            groups(sp, group)
            for i in range(NB_OP):
                n_loads = len([g for g in range(GROUPS + 1) if g % 3 == i])
                sp.wait_ge(k_in[i], n_loads * 16 * 9)
                sp.wait_ge(v_in_s[i], n_loads * 16)
            for half in range(2):
                sp.wait_ge(s["fin_ok"], half + 1)
                ring = (B - 1) % 2 * NK + 4 * half
                rows = ((B - 1) * NK + 4 * half) * P
                sp.dma_start(out[rows:rows + 4 * P].rearrange("(q p) d -> p q d", p=P),
                             att[:, ring:ring + 4]).then_inc(s["fin_st"], 16)
            sp.wait_ge(s["fin_st"], 32)

        @block.gpsimd
        def _(pool):
            g_ = nc.gpsimd
            for i in range(NB_OP):
                g_.memset(q_op[i][QR:96].bitcast(F32), 1.0).then_inc(s["init"], 1)
            pool.wait_ge(s["init"], NB_OP)
            for i in range(NB_OP):
                g_.memset(v_op[i][:], 1.0).then_inc(s["init_v"], 1)
            g_.tensor_copy(slot_i[:], slot[:]).then_inc(s["pool_c"], 1)
            pool.wait_ge(s["pool_c"], 1)
            pool.wait_ge(s["w_ready"], 1)
            for i in range(2):
                pool.dma_start(scratch["credit"][i], wts[:, 0, 0:1]).then_inc(s[f"o_st{i}"], 16)

            CPB = 7

            def combine(n, u, turn, ring):
                c = Chain(pool, s["pool_c"], n * CPB + 1, s["passed"])
                pool.dma_start(base_c[u][:], scratch["base"][ds(n * P, P)]).then_inc(s[f"base_in{u}"], 16)
                c.link(g_.tensor_copy(col_w[u][:], wts[:, :, ds(n, 1)].rearrange("p a o -> p (a o)")))
                c.link(g_.tensor_copy(col_i[u][:], slot_i[:, :, ds(n, 1)].rearrange("p a o -> p (a o)")))
                for k in range(2):
                    g_.indirect_dma_start(y_c[k][u][:], None, scratch["yr"],
                                          bass.IndirectOffsetOnAxis(col_i[u][:, k:k + 1], 0)).then_inc(s[f"yg_in{u}"], 16)
                hold(pool, s[f"base_in{u}"], 16 * (turn + 1), s["passed"])
                hold(pool, s[f"o_st{u}"], 16 * (turn + 1), s["passed"])
                acc = base_c[u]
                c.link(g_.tensor_tensor(acc[:], acc[:], att[:, ds(ring, 1)].rearrange("p o d -> p (o d)"), ALU.add))
                hold(pool, s[f"yg_in{u}"], 32 * (turn + 1), s["passed"])
                for k in range(2):
                    y = y_c[k][u]
                    c.link(g_.tensor_scalar(y[:], y[:], col_w[u][:, k:k + 1], None, ALU.mult))
                    c.link(g_.tensor_tensor(acc[:], acc[:], y[:], ALU.add))
                assert c.k == CPB
                pool.sem_inc(s["c_ok"], 1)
                pool.dma_start(out[ds(n * P, P)], acc[:]).then_inc(s[f"o_st{u}"], 16)

            GB = H // GH
            with pool.Fori(0, B - 1) as b:
                hold(pool, s["att_ok"], b * (GB * 2) + GB * 2, s["passed"])
                with pool.Fori(0, NK // 2) as i:
                    for u in range(2):
                        combine(b * NK + i * 2 + u, u, b * (NK // 2) + i, (b % 2) * NK + i * 2 + u)
            first = (B - 1) * NK
            pool.dma_start(fin[:, 0], scratch["base"][first * P:].rearrange("(q p) d -> p q d", p=P)).then_inc(s["fin_base"], 16)
            for q in range(NK):
                for k in range(2):
                    g_.indirect_dma_start(fin[:, 1 + k, q], None, scratch["yr"],
                                          bass.IndirectOffsetOnAxis(slot_i[:, k, first + q:first + q + 1], 0)
                                          ).then_inc(s["fin_y"], 16)
            for i in range(2):
                pool.wait_ge(s[f"o_st{i}"], 16 * ((B - 1) * NK // 2 + 1))

        @block.vector
        def _(dve):
            v = nc.vector
            c = Chain(dve, s["dve_w"])
            lg = logits[:].rearrange("p (n e) -> p n e", e=E)
            wide = lambda a: a[:, :, None].to_broadcast([P, NBLK, E])
            c.link(v.tensor_reduce(t64[:], lg, AX.X, ALU.max))
            v.tensor_tensor(ex[:], lg, wide(t64), ALU.subtract).then_inc(s["sub_ok"], 1)

            def weights():
                dve.wait_ge(s["ex_ok"], 1)
                c.link(v.tensor_reduce(z64[:], ex[:], AX.X, ALU.add))
                c.link(v.reciprocal(t64[:], z64[:]))
                c.link(v.tensor_tensor(ex[:], ex[:], wide(t64), ALU.mult))
                em = em8[:, None, :].to_broadcast([P, NBLK, E])
                for k in range(2):
                    c.link(v.tensor_tensor(cmp_[:], em, wide(pick[:, k]), ALU.is_equal))
                    c.link(v.tensor_tensor(cmp_[:], cmp_[:], ex[:], ALU.mult))
                    c.link(v.tensor_reduce(wts[:, k], cmp_[:], AX.X, ALU.add))
                c.link(v.tensor_tensor(t64[:], wts[:, 0], wts[:, 1], ALU.add))
                c.link(v.tensor_scalar(t64[:], t64[:], 1e-20, None, ALU.add))
                c.link(v.reciprocal(z64[:], t64[:]))
                for k in range(2):
                    ins = v.scalar_tensor_tensor(wts[:, k], wts[:, k], ROUTE_SCALE, z64[:], ALU.mult, ALU.mult)
                ins.then_inc(s["w_ready"], 1)

            dve.sem_inc(s["c_ok"], 2 * NK)
            dve.sem_inc(s["s1_read"], 2)

            def max_unit(use, bank, w):
                dve.wait_ge(s["s1_ps"], use + 1)
                v.tensor_reduce(neg[w // CHUNK % 2][:, w % CHUNK:w % CHUNK + 1], p1[bank][:], AX.X, ALU.max,
                                negate=True).then_inc(s["s1_read"], 1)

            def output(g, half, use, bank):
                x_no = g * 2 + half
                b, hg = g // (H // GH), g % (H // GH)
                dve.wait_ge(s["s1_ps"], use + 1)
                ot = p1[bank][:, 0:512].rearrange("p (q h c) -> p q h c", q=4, h=GH)
                v.reciprocal(rec[:], ot[:, :, :, HD]).then_inc(s["rec_ok"], 1)
                dve.wait_ge(s["c_ok"], b * NK + NK)
                dve.wait_ge(s["rec_ok"], x_no + 1)
                dst = att[:, ds((b % 2) * NK + 4 * half, 4), ds(hg * (GH * HD), GH * HD)]
                v.tensor_tensor(dst.rearrange("p q (h c) -> p q h c", h=GH), ot[:, :, :, 0:HD],
                                rec[:, :, :, None].to_broadcast([P, 4, GH, HD]), ALU.mult).then_inc(s["att_ok"], 1)
                dve.wait_ge(s["att_ok"], x_no + 1)
                dve.sem_inc(s["s1_read"], 1)

            def last_terms():
                cf = Chain(dve, s["dve_f"])
                dve.wait_ge(s["fin_base"], 16)
                dve.wait_ge(s["fin_y"], 16 * 2 * NK)
                for k in range(2):
                    for q in range(NK):
                        n = (B - 1) * NK + q
                        ins = v.scalar_tensor_tensor(fin[:, 0, q], fin[:, 1 + k, q], wts[:, k, n:n + 1],
                                                     fin[:, 0, q], ALU.mult, ALU.add)
                    cf.link(ins)

            def final(half):
                ring = (B - 1) % 2 * NK + 4 * half
                acc = att[:, ring:ring + 4]
                v.tensor_tensor(acc, acc, fin[:, 0, 4 * half:4 * half + 4], ALU.add).then_inc(s["fin_ok"], 1)

            for w in range(MAX_UNITS):
                max_unit(w, w % 2, w)
            weights()

            def group(g, u, turn, has_prev, has_next):
                base, r, w = ring1(g, not has_prev), 0, 0
                for n in range(UNITS):
                    if has_next:
                        while w < AHEAD[n]:
                            max_unit(base + r, bank1(not has_prev, r), w)
                            w, r = w + 1, r + 1
                    if n % HALF == OUT_TURN and (n >= HALF or has_prev):
                        pg, ph = (g, 0) if n >= HALF else (g - 1, 1)
                        output(pg, ph, base + r, bank1(not has_prev, r))
                        r += 1
                    if n == HALF - 1 and not has_next:
                        last_terms()
                if not has_next:
                    final(0)
                    output(g, 1, base + r, bank1(not has_prev, r))
                    final(1)

            groups(dve, group)

        @block.scalar
        def _(act):
            a = nc.scalar
            act.wait_ge(s["sub_ok"], 1)
            a.activation(ex[:], ex[:], ACT.Exp).then_inc(s["ex_ok"], 1)
            act.sem_inc(s["s2_read"], 3)
            act.sem_inc(s["o_ok"], 1)
            act.sem_inc(s["pv_done"], NK)

            def row_copy(g, use, bank, c):
                act.wait_ge(s["s2_ps"], use + 1)
                if c >= 4 or not (isinstance(g, int) and g == 0):
                    act.wait_ge(m_in[c % 4], g * 32 + 16 * (c // 4))
                a.copy(m_row[c % 4][:], p2[bank][0:4, 0:P]).then_inc(s["s2_read"], 1)
                act.wait_ge(s["s2_read"], use + 4)
                act.sem_inc(s["m_ok"], 1)

            def spread_v(g, u, turn):
                act.wait_ge(v_in_s[u], 16 * (turn + 1))
                a.copy(v_op[u][:, :, :, 0:HD], v_in[u][:].rearrange("p k (h d) -> p k h d", h=GH)).then_inc(s["v_ok"], 1)

            def output_copy(g, half):
                act.wait_ge(s["pv_done"], (g * 2 + half) * NK + 2 * NK)
                a.copy(o_sb[half][:], p_o[:]).then_inc(s["o_ok"], 1)

            act.wait_ge(s["init_v"], NB_OP)
            spread_v(0, 0, 0)
            for c in range(CHUNKS - 1):
                row_copy(0, c, c % 3, c)

            def group(g, u, turn, has_prev, has_next):
                base, r = ring2(g), 0
                nu, nt = following(u, turn)
                for n in range(UNITS):
                    half, kb, h = n // HALF, n % HALF // GH, n % GH
                    act.wait_ge(s["s2_ps"], base + (r + 1))
                    if h == 0:
                        act.wait_ge(s["pv_done"], g * (2 * NK) + (half * NK + kb - 3 + NK))
                    a.activation(probs[kb % 4][:, h], p2[bank2(r)][:], ACT.Exp).then_inc(s["s2_read"], 1)
                    r += 1
                    if n == OWN_TURN:
                        row_copy(g, base + r, bank2(r), CHUNKS - 1)
                        r += 1
                    elif n in TURN_AT and has_next:
                        row_copy(g + 1, base + r, bank2(r), TURN_AT[n])
                        r += 1
                    if n % HALF == OUT_COPY and (n >= HALF or has_prev):
                        output_copy(*((g, 0) if n >= HALF else (g - 1, 1)))
                    if n == V_SPREAD and has_next:
                        spread_v(g + 1, nu, nt)
                if not has_next:
                    output_copy(g, 1)

            groups(act, group)

        @block.tensor
        def _(pe):
            t = nc.tensor

            def max_unit(u, use, bank, w):
                chunk, r = divmod(w, CHUNK)
                half, h = divmod(chunk, GH)
                qb = 4 * half + r
                pe.wait_ge(s["s1_read"], use + 1)
                for kh in range(2):
                    ins = t.matmul(p1[bank][:, kh * 512:(kh + 1) * 512], q_op[u][0:S1_ROWS, h, qb * P:(qb + 1) * P],
                                   k_op[u][0:S1_ROWS, h, kh * 512:(kh + 1) * 512], start=True, stop=True)
                ins.then_inc(s["s1_ps"], 1)

            def turn_max(read, use, bank, c):
                pe.wait_ge(s["s1_read"], read)
                pe.wait_ge(s["s2_read"], use + 1)
                t.transpose(p2[bank][0:4, 0:P], neg[c % 2][:].bitcast(F32), ident[:]).then_inc(s["s2_ps"], 1)

            def score_unit(g, u, use, bank, n):
                half, kb, h = n // HALF, n % HALF // GH, n % GH
                pe.wait_ge(s["s2_read"], use + 1)
                if kb == 0:
                    pe.wait_ge(m_in[h], g * 32 + 16 * (half + 1))
                t.matmul(p2[bank][:], k_op[u][0:S2_ROWS, h, kb * P:(kb + 1) * P],
                         q_op[u][0:S2_ROWS, h, half * HQ:(half + 1) * HQ], start=True, stop=True).then_inc(s["s2_ps"], 1)

            def products(g, u, half, kb, read):
                pe.wait_ge(s["s2_read"], read)
                if kb == 0:
                    pe.wait_ge(s["v_ok"], g + 1)
                    pe.wait_ge(s["o_ok"], g * 2 + (half + 1))
                for h in range(GH):
                    ins = t.matmul(p_o[32 * h:32 * h + 32], v_op[u][:, kb, h], probs[kb % 4][:, h],
                                   start=(kb == 0), stop=(kb == NK - 1))
                ins.then_inc(s["pv_done"], 1)

            def turn_output(g, half, use, bank):
                pe.wait_ge(s["o_ok"], g * 2 + (half + 2))
                pe.wait_ge(s["s1_read"], use + 1)
                for q in range(4):
                    ins = t.transpose(p1[bank][:, q * P:(q + 1) * P], o_sb[half][:, q * P:(q + 1) * P], ident[:])
                ins.then_inc(s["s1_ps"], 1)

            pe.wait_ge(s["ones_in"], 16 * NB_OP)
            pe.wait_ge(k_in[0], 16 * 9)
            pe.wait_ge(s["init"], 1)
            for w in range(MAX_UNITS):
                max_unit(0, w, w % 2, w)
                if w % CHUNK == 1 and w >= CHUNK:
                    c = w // CHUNK - 1
                    turn_max(CHUNK * (c + 1) + 2, c, c % 3, c)
            pe.wait_ge(s["init"], NB_OP)

            def group(g, u, turn, has_prev, has_next):
                b1, r1, w = ring1(g, not has_prev), 0, 0
                b2, r2 = ring2(g), 0
                nu, nt = following(u, turn)
                read = {}
                maxed = {}
                for n in range(UNITS):
                    score_unit(g, u, b2 + r2, bank2(r2), n)
                    read[n] = b2 + (r2 + 4)
                    r2 += 1
                    if has_next:
                        if n == 0:
                            pe.wait_ge(k_in[nu], (nt + 1) * (16 * 9))
                        while w < AHEAD[n]:
                            max_unit(nu, b1 + r1, bank1(not has_prev, r1), w)
                            maxed[w] = b1 + (r1 + 3)
                            w, r1 = w + 1, r1 + 1
                        if n in TURN_AT:
                            turn_max(maxed[CHUNK * (TURN_AT[n] + 1) - 1], b2 + r2, bank2(r2), TURN_AT[n])
                            r2 += 1
                    if n == OWN_TURN:
                        turn_max(b1 + 2, b2 + r2, bank2(r2), CHUNKS - 1)
                        r2 += 1
                    half, l = divmod(n, HALF)
                    if l == 2 and half == 0 and has_prev:
                        products(g - 1, (u + 2) % 3, 1, NK - 1, b2 + 2)
                    elif l % GH == 2 and n != 2:
                        kb = l // GH - 1
                        if kb >= 0:
                            products(g, u, half, kb, read[n - 3])
                        else:
                            products(g, u, 0, NK - 1, read[n - 3])
                    if l == OUT_TURN and (half or has_prev):
                        turn_output(*((g, 0) if half else (g - 1, 1)), b1 + r1, bank1(not has_prev, r1))
                        r1 += 1
                if not has_next:
                    products(g, u, 1, NK - 1, read[UNITS - 1])
                    turn_output(g, 1, b1 + r1, bank1(not has_prev, r1))

            groups(pe, group)


def kernel(L0_attn_x, L0_attn_W_kqv, L0_ffn_gate_w, L0_ffn_w_gate, L0_ffn_w_up, L0_ffn_w_down,
           L0_ffn_sw_gate, L0_ffn_sw_up, L0_ffn_sw_down):
    import concourse.bacc as bacc
    from concourse.bass_utils import run_bass_kernel_spmd

    f32 = np.float32
    ratio = (2 ** 8) ** (1.0 / H)
    slopes = np.array([1.0 / ratio ** (i + 1) for i in range(H)], dtype=f32)
    bias = slopes[:, None] * (np.arange(S) - (S - 1)).astype(f32)[None, :]
    top = (bias.view(np.uint32) & np.uint32(0xFFFFF000)).view(f32)
    ali = np.zeros((H + 1, 2, S), f32)
    ali[:H, 0], ali[:H, 1], ali[H] = top, bias - top, 1.0
    arrays = {
        "x": np.ascontiguousarray(L0_attn_x).reshape(T, D),
        "wqkv": np.ascontiguousarray(np.asarray(L0_attn_W_kqv).T),
        "gate_wt": np.ascontiguousarray(np.asarray(L0_ffn_gate_w).T),
        "w_gate": np.ascontiguousarray(L0_ffn_w_gate),
        "w_up": np.ascontiguousarray(L0_ffn_w_up),
        "w_down": np.ascontiguousarray(L0_ffn_w_down),
        "sw_gate": np.ascontiguousarray(L0_ffn_sw_gate),
        "sw_up": np.ascontiguousarray(L0_ffn_sw_up),
        "sw_down": np.ascontiguousarray(L0_ffn_sw_down),
        "ident": np.eye(P, dtype=f32),
        "tri": np.triu(np.ones((P, P), f32), 1),
        "ali": ali,
    }
    nc = bacc.Bacc("TRN2", target_bir_lowering=False, num_devices=1)
    args = [nc.dram_tensor(f"in_{k}", a.shape, mybir.dt.from_np(a.dtype), kind="ExternalInput").ap()
            for k, a in arrays.items()]
    out = nc.dram_tensor("out_0", (T, D), F32, kind="ExternalOutput").ap()
    build(nc, *args, out)
    r = run_bass_kernel_spmd(nc, [{f"in_{k}": a for k, a in arrays.items()}], core_ids=[0])
    return r.results[0]["out_0"].reshape(B, S, D)
```
